# Optimizing a Trainium2 kernel written in Bass

```python
import numpy as np
import jax
import jax.numpy as jnp

def _softmax(x, axis=-1):
    return jax.nn.softmax(x, axis=axis)

def _gelu(x):
    return jax.nn.gelu(x, approximate=True)

def _silu(x):
    return jax.nn.silu(x)

def _sigmoid(x):
    return jax.nn.sigmoid(x)

def _layernorm(x, axis=-1, eps=1e-05):
    m = jnp.mean(x, axis=axis, keepdims=True)
    v = jnp.var(x, axis=axis, keepdims=True)
    return (x - m) / jnp.sqrt(v + eps)

def _scatter_add(tgt, idx, src, axis=0):
    return tgt.at[idx].add(src)

def _segment_sum(src, seg, n):
    return jax.ops.segment_sum(src, seg, n)
kernel_name = 'mk_xattn_seq_d1_seqx_r4_c247e5'

def setup_inputs(seed: int=0):
    np.random.seed(seed)
    _w = jnp.asarray

    def _rec_inputs():
        import jax
        import jax.numpy as jnp
        _rk = jax.random.key(seed)
        x = 7.22e-05 + 1 * jax.random.normal(jax.random.fold_in(_rk, 1), (64, 128, 512), jnp.float32)
        _lenS = 128 - jax.random.randint(jax.random.fold_in(_rk, 7), (64,), 0, max(1, 128 // 4) + 1, jnp.int32)
        _lenS2 = 128 - jax.random.randint(jax.random.fold_in(_rk, 8), (64,), 0, max(1, 128 // 4) + 1, jnp.int32)
        _ctx_2048P = jax.random.normal(jax.random.fold_in(_rk, 11), (64, 16, 512), jnp.float32)
        _ctx_2048c = jax.random.dirichlet(jax.random.fold_in(_rk, 511), 0.3 * jnp.ones((16,), jnp.float32), (64, 128))
        _ctx_2048t = jnp.einsum('bsk,bkd->bsd', _ctx_2048c, _ctx_2048P)
        _ctx_2048t = _ctx_2048t * jax.lax.rsqrt(jnp.mean(jnp.square(_ctx_2048t)) + 1e-12) * 0.953939
        ctx_2048 = 3.03215e-05 + 0.0999827 * (_ctx_2048t + 0.3 * jax.random.normal(jax.random.fold_in(_rk, 611), (64, 128, 512), jnp.float32))
        return (x, ctx_2048)
    x, ctx_2048 = _rec_inputs()

    def _L0_xattn_setup():
        import jax, jax.numpy as jnp
        import numpy as np
        N_HEAD = 32
        EPS = 1e-05

        def _ln(x, w, b):
            m = jnp.mean(x, axis=-1, keepdims=True)
            v = jnp.mean((x - m) ** 2, axis=-1, keepdims=True)
            return (x - m) * jax.lax.rsqrt(v + EPS) * w + b

        def _forward(x, state, i, ln1_w, ln1_b, ln2_w, ln2_b, maa_x, maa_w, maa_k, maa_v, maa_r, maa_g, maa_w1, maa_w2, time_decay, decay_w1, decay_w2, faaaa, Wr, Wk, Wv, Wg, Wo, gn_w, gn_b, fmaa_k, fmaa_r, fWk, fWr, fWv):
            B, L, C = x.shape
            H = N_HEAD
            S = C // H
            i0 = (2 + S) * i
            xa = _ln(x, ln1_w, ln1_b)
            sx = jnp.concatenate([state[:, i0 + 1][:, None], xa[:, :-1]], axis=1) - xa
            xxx = xa + sx * maa_x
            t = jnp.tanh(xxx @ maa_w1).reshape(B, L, 5, -1)
            m = jnp.einsum('blfd,fdc->blfc', t, maa_w2)
            mw, mk, mv, mr, mg = (m[:, :, j] for j in range(5))
            xw = xa + sx * (maa_w + mw)
            xk = xa + sx * (maa_k + mk)
            xv = xa + sx * (maa_v + mv)
            xr = xa + sx * (maa_r + mr)
            xg = xa + sx * (maa_g + mg)
            w = time_decay + jnp.tanh(xw @ decay_w1) @ decay_w2
            w = jnp.exp(-jnp.exp(w)).reshape(B, L, H, S)
            r = (xr @ Wr.T).reshape(B, L, H, S)
            k = (xk @ Wk.T).reshape(B, L, H, S)
            v = (xv @ Wv.T).reshape(B, L, H, S)
            g = jax.nn.silu(xg @ Wg.T)
            s0 = state[:, i0 + 2:i0 + 2 + S].reshape(B, H, S, S)

            def step(s, inp):
                k_l, v_l, w_l, r_l = inp
                a = k_l[..., :, None] * v_l[..., None, :]
                out = jnp.einsum('bhs,bhst->bht', r_l, faaaa * a + s)
                s_new = a + w_l[..., None] * s
                return (s_new, out)
            seq = tuple((z.transpose(1, 0, 2, 3) for z in (k, v, w, r)))
            _, outs = jax.lax.scan(step, s0, seq)
            y = outs.transpose(1, 0, 2, 3)
            gm = jnp.mean(y, axis=-1, keepdims=True)
            gv = jnp.mean((y - gm) ** 2, axis=-1, keepdims=True)
            y = ((y - gm) * jax.lax.rsqrt(gv + EPS)).reshape(B, L, C) * gn_w + gn_b
            x = x + y * g @ Wo.T
            xc = _ln(x, ln2_w, ln2_b)
            sxc = jnp.concatenate([state[:, i0][:, None], xc[:, :-1]], axis=1) - xc
            xk2 = xc + sxc * fmaa_k
            xr2 = xc + sxc * fmaa_r
            rr = jax.nn.sigmoid(xr2 @ fWr.T)
            kk = jnp.square(jax.nn.relu(xk2 @ fWk.T))
            x = x + rr * (kk @ fWv.T)
            return x
        key = jax.random.key(seed)
        B, L, C, H = (8, 128, 512, N_HEAD)
        S = C // H
        DM, DD = (32, 64)
        ks = jax.random.split(key, 32)
        n = lambda k, shp, s=1.0: jax.random.normal(k, shp, dtype=jnp.float32) * s
        u = lambda k, shp: jax.random.uniform(k, shp, dtype=jnp.float32)
        inp = {'x': n(ks[0], (B, L, C)), 'state': n(ks[1], (B, 2 + S, C), 0.1), 'i': 0, 'ln1_w': jnp.ones((C,), jnp.float32), 'ln1_b': jnp.zeros((C,), jnp.float32), 'ln2_w': jnp.ones((C,), jnp.float32), 'ln2_b': jnp.zeros((C,), jnp.float32), 'maa_x': u(ks[2], (C,)), 'maa_w': u(ks[3], (C,)), 'maa_k': u(ks[4], (C,)), 'maa_v': u(ks[5], (C,)), 'maa_r': u(ks[6], (C,)), 'maa_g': u(ks[7], (C,)), 'maa_w1': n(ks[8], (C, 5 * DM), 0.02), 'maa_w2': n(ks[9], (5, DM, C), 0.02), 'time_decay': n(ks[10], (C,), 0.5), 'decay_w1': n(ks[11], (C, DD), 0.02), 'decay_w2': n(ks[12], (DD, C), 0.02), 'faaaa': n(ks[13], (H, S, 1), 0.1), 'Wr': n(ks[14], (C, C), 0.02), 'Wk': n(ks[15], (C, C), 0.02), 'Wv': n(ks[16], (C, C), 0.02), 'Wg': n(ks[17], (C, C), 0.02), 'Wo': n(ks[18], (C, C), 0.02), 'gn_w': jnp.ones((C,), jnp.float32), 'gn_b': jnp.zeros((C,), jnp.float32), 'fmaa_k': u(ks[19], (C,)), 'fmaa_r': u(ks[20], (C,)), 'fWk': n(ks[21], (C, C), 0.02), 'fWr': n(ks[22], (C, C), 0.02), 'fWv': n(ks[23], (C, C), 0.02)}
        return inp
    _L0_xattn_all = _L0_xattn_setup()
    _L0_xattn_in = {k: v for k, v in _L0_xattn_all.items() if k in ('ln1_w', 'ln1_b', 'ln2_w', 'ln2_b', 'maa_x', 'maa_w', 'maa_k', 'maa_v', 'maa_r', 'maa_g', 'maa_w1', 'maa_w2', 'time_decay', 'decay_w1', 'decay_w2', 'faaaa', 'Wr', 'Wk', 'Wv', 'Wg', 'Wo', 'gn_w', 'gn_b', 'fmaa_k', 'fmaa_r', 'fWk', 'fWr', 'fWv')}
    del _L0_xattn_all
    return {'x': x, 'ctx_2048': ctx_2048, 'L0_xattn_ln1_w': _L0_xattn_in['ln1_w'], 'L0_xattn_ln1_b': _L0_xattn_in['ln1_b'], 'L0_xattn_ln2_w': _L0_xattn_in['ln2_w'], 'L0_xattn_ln2_b': _L0_xattn_in['ln2_b'], 'L0_xattn_maa_x': _L0_xattn_in['maa_x'], 'L0_xattn_maa_w': _L0_xattn_in['maa_w'], 'L0_xattn_maa_k': _L0_xattn_in['maa_k'], 'L0_xattn_maa_v': _L0_xattn_in['maa_v'], 'L0_xattn_maa_r': _L0_xattn_in['maa_r'], 'L0_xattn_maa_g': _L0_xattn_in['maa_g'], 'L0_xattn_maa_w1': _L0_xattn_in['maa_w1'], 'L0_xattn_maa_w2': _L0_xattn_in['maa_w2'], 'L0_xattn_time_decay': _L0_xattn_in['time_decay'], 'L0_xattn_decay_w1': _L0_xattn_in['decay_w1'], 'L0_xattn_decay_w2': _L0_xattn_in['decay_w2'], 'L0_xattn_faaaa': _L0_xattn_in['faaaa'], 'L0_xattn_Wr': _L0_xattn_in['Wr'], 'L0_xattn_Wk': _L0_xattn_in['Wk'], 'L0_xattn_Wv': _L0_xattn_in['Wv'], 'L0_xattn_Wg': _L0_xattn_in['Wg'], 'L0_xattn_Wo': _L0_xattn_in['Wo'], 'L0_xattn_gn_w': _L0_xattn_in['gn_w'], 'L0_xattn_gn_b': _L0_xattn_in['gn_b'], 'L0_xattn_fmaa_k': _L0_xattn_in['fmaa_k'], 'L0_xattn_fmaa_r': _L0_xattn_in['fmaa_r'], 'L0_xattn_fWk': _L0_xattn_in['fWk'], 'L0_xattn_fWr': _L0_xattn_in['fWr'], 'L0_xattn_fWv': _L0_xattn_in['fWv']}

def reference(x, ctx_2048, L0_xattn_ln1_w, L0_xattn_ln1_b, L0_xattn_ln2_w, L0_xattn_ln2_b, L0_xattn_maa_x, L0_xattn_maa_w, L0_xattn_maa_k, L0_xattn_maa_v, L0_xattn_maa_r, L0_xattn_maa_g, L0_xattn_maa_w1, L0_xattn_maa_w2, L0_xattn_time_decay, L0_xattn_decay_w1, L0_xattn_decay_w2, L0_xattn_faaaa, L0_xattn_Wr, L0_xattn_Wk, L0_xattn_Wv, L0_xattn_Wg, L0_xattn_Wo, L0_xattn_gn_w, L0_xattn_gn_b, L0_xattn_fmaa_k, L0_xattn_fmaa_r, L0_xattn_fWk, L0_xattn_fWr, L0_xattn_fWv):
    import jax
    import jax.numpy as jnp

    def _L0_xattn_ref(x, state, i, ln1_w, ln1_b, ln2_w, ln2_b, maa_x, maa_w, maa_k, maa_v, maa_r, maa_g, maa_w1, maa_w2, time_decay, decay_w1, decay_w2, faaaa, Wr, Wk, Wv, Wg, Wo, gn_w, gn_b, fmaa_k, fmaa_r, fWk, fWr, fWv):
        import jax, jax.numpy as jnp
        import numpy as np
        N_HEAD = 32
        EPS = 1e-05

        def _ln(x, w, b):
            m = jnp.mean(x, axis=-1, keepdims=True)
            v = jnp.mean((x - m) ** 2, axis=-1, keepdims=True)
            return (x - m) * jax.lax.rsqrt(v + EPS) * w + b

        def _forward(x, state, i, ln1_w, ln1_b, ln2_w, ln2_b, maa_x, maa_w, maa_k, maa_v, maa_r, maa_g, maa_w1, maa_w2, time_decay, decay_w1, decay_w2, faaaa, Wr, Wk, Wv, Wg, Wo, gn_w, gn_b, fmaa_k, fmaa_r, fWk, fWr, fWv):
            B, L, C = x.shape
            H = N_HEAD
            S = C // H
            i0 = (2 + S) * i
            xa = _ln(x, ln1_w, ln1_b)
            sx = jnp.concatenate([state[:, i0 + 1][:, None], xa[:, :-1]], axis=1) - xa
            xxx = xa + sx * maa_x
            t = jnp.tanh(xxx @ maa_w1).reshape(B, L, 5, -1)
            m = jnp.einsum('blfd,fdc->blfc', t, maa_w2)
            mw, mk, mv, mr, mg = (m[:, :, j] for j in range(5))
            xw = xa + sx * (maa_w + mw)
            xk = xa + sx * (maa_k + mk)
            xv = xa + sx * (maa_v + mv)
            xr = xa + sx * (maa_r + mr)
            xg = xa + sx * (maa_g + mg)
            w = time_decay + jnp.tanh(xw @ decay_w1) @ decay_w2
            w = jnp.exp(-jnp.exp(w)).reshape(B, L, H, S)
            r = (xr @ Wr.T).reshape(B, L, H, S)
            k = (xk @ Wk.T).reshape(B, L, H, S)
            v = (xv @ Wv.T).reshape(B, L, H, S)
            g = jax.nn.silu(xg @ Wg.T)
            s0 = state[:, i0 + 2:i0 + 2 + S].reshape(B, H, S, S)

            def step(s, inp):
                k_l, v_l, w_l, r_l = inp
                a = k_l[..., :, None] * v_l[..., None, :]
                out = jnp.einsum('bhs,bhst->bht', r_l, faaaa * a + s)
                s_new = a + w_l[..., None] * s
                return (s_new, out)
            seq = tuple((z.transpose(1, 0, 2, 3) for z in (k, v, w, r)))
            _, outs = jax.lax.scan(step, s0, seq)
            y = outs.transpose(1, 0, 2, 3)
            gm = jnp.mean(y, axis=-1, keepdims=True)
            gv = jnp.mean((y - gm) ** 2, axis=-1, keepdims=True)
            y = ((y - gm) * jax.lax.rsqrt(gv + EPS)).reshape(B, L, C) * gn_w + gn_b
            x = x + y * g @ Wo.T
            xc = _ln(x, ln2_w, ln2_b)
            sxc = jnp.concatenate([state[:, i0][:, None], xc[:, :-1]], axis=1) - xc
            xk2 = xc + sxc * fmaa_k
            xr2 = xc + sxc * fmaa_r
            rr = jax.nn.sigmoid(xr2 @ fWr.T)
            kk = jnp.square(jax.nn.relu(xk2 @ fWk.T))
            x = x + rr * (kk @ fWv.T)
            return x
        return _forward(x, state, i, ln1_w, ln1_b, ln2_w, ln2_b, maa_x, maa_w, maa_k, maa_v, maa_r, maa_g, maa_w1, maa_w2, time_decay, decay_w1, decay_w2, faaaa, Wr, Wk, Wv, Wg, Wo, gn_w, gn_b, fmaa_k, fmaa_r, fWk, fWr, fWv)
    x = _L0_xattn_ref(x, ctx_2048, 0, L0_xattn_ln1_w, L0_xattn_ln1_b, L0_xattn_ln2_w, L0_xattn_ln2_b, L0_xattn_maa_x, L0_xattn_maa_w, L0_xattn_maa_k, L0_xattn_maa_v, L0_xattn_maa_r, L0_xattn_maa_g, L0_xattn_maa_w1, L0_xattn_maa_w2, L0_xattn_time_decay, L0_xattn_decay_w1, L0_xattn_decay_w2, L0_xattn_faaaa, L0_xattn_Wr, L0_xattn_Wk, L0_xattn_Wv, L0_xattn_Wg, L0_xattn_Wo, L0_xattn_gn_w, L0_xattn_gn_b, L0_xattn_fmaa_k, L0_xattn_fmaa_r, L0_xattn_fWk, L0_xattn_fWr, L0_xattn_fWv)
    return x

_drawn_inputs = setup_inputs


def setup_inputs(seed=0):
    import zlib

    import numpy as np

    out = dict(_drawn_inputs(seed))
    spreads = {'L0_xattn_ln1_w': (1.0, 0.2),
     'L0_xattn_ln1_b': (0.0, 0.1),
     'L0_xattn_ln2_w': (1.0, 0.6),
     'L0_xattn_ln2_b': (0.0, 0.8),
     'L0_xattn_gn_w': (1.0, 0.6),
     'L0_xattn_gn_b': (0.0, 0.8)}
    factors = {'ctx_2048': 17.369,
     'L0_xattn_maa_x': 6.585,
     'L0_xattn_maa_w': 8.0,
     'L0_xattn_maa_w1': 3.419,
     'L0_xattn_maa_w2': 3.423,
     'L0_xattn_decay_w1': 8.0,
     'L0_xattn_decay_w2': 8.0,
     'L0_xattn_faaaa': 3.672,
     'L0_xattn_fmaa_r': 8.0,
     'L0_xattn_fWr': 7.513}
    for name, (base, spread) in spreads.items():
        noise = np.random.default_rng([zlib.crc32(name.encode()), seed]).standard_normal(out[name].shape)
        drawn = base * np.exp(spread * noise) if base else spread * noise
        out[name] = jnp.asarray(drawn.astype(out[name].dtype))
    for name, factor in factors.items():
        out[name] = (out[name] * factor).astype(out[name].dtype)
    return out
```

```python
from contextlib import ExitStack

import concourse.bass as bass
from concourse import mybir

F32 = mybir.dt.float32
ALU = mybir.AluOpType
ACT = mybir.ActivationFunctionType

P = 128
GB = 4
T = GB * P
CT = 4
C = CT * P
S = 16
HT = P // S
DM, DD = 32, 64
EPS = 1e-5
NF = 5
BANKS = 3
STEPS = CT * S
RING = 4

VECS = ["ln1_w", "ln1_b", "ln2_w", "ln2_b", "maa_x", "maa_w", "maa_k", "maa_v", "maa_r", "maa_g",
        "time_decay", "faaaa", "gn_w", "gn_b", "fmaa_k", "fmaa_r"]
MATS = ["Wr", "Wk", "Wv", "Wg", "Wo", "fWk", "fWr", "fWv"]
SELS = ["ident", "spread", "gather", "headsum", "center", "headmean"]
SELW = {"ident": P, "spread": 4 * P, "gather": 4 * 32, "headsum": P, "center": P, "headmean": P}


def general_uses():
    uses = [("state", "act")] + [(f"tr1_{c}", "act") for c in range(CT)] + [("lora0", "act"), ("lora1", "act")]

    def mix(f):
        return [(f"mix{f}_{c}", "dve") for c in range(CT)]

    def proj(f):
        return [(f"proj{f}_{c}", "act") for c in range(CT)]
    uses += mix(0) + mix(1) + [("decay_in", "act")] + proj(0) + mix(2) + proj(1) + mix(3) + proj(2)
    uses += mix(4) + proj(3) + proj(4)
    for c in range(CT):
        uses += [(f"bonus_{c}", "dve"), (f"center_{c}", "dve"), (f"var_{c}", "act")]
    uses += [(f"wo_{b}", "dve") for b in range(GB)] + [(f"tr2_{c}", "act") for c in range(CT)]
    uses += [(f"key_{c}", "act") for c in range(CT)]
    for b in range(GB):
        uses += [(f"recept_{b}", "act"), (f"value_{b}", "dve")]
    return uses


def rwkv_kernel(nc, x, ctx_in, vecs, mats, maa_w1, maa_w2, decay_w1, decay_w2, sels, out):
    NB = x.shape[0]
    NG = NB // GB
    uses = general_uses()
    order = {name: n for n, (name, _) in enumerate(uses)}
    who = dict(uses)
    rank = {name: sum(w == who[name] for _, w in uses[:n]) for name, n in order.items()}
    per = {w: sum(u[1] == w for u in uses) for w in ("act", "dve")}

    with ExitStack() as ctx:
        def sb(name, shape):
            return ctx.enter_context(nc.sbuf_tensor(name, shape, F32))

        def sem(name):
            return ctx.enter_context(nc.semaphore(name))

        vec = sb("vec", [P, len(VECS), CT])
        mat = {n: sb("m_" + n, [P, CT, C]) for n in MATS}
        w1 = sb("w1", [P, CT, NF * DM])
        w2a = sb("w2a", [4 * DM, C])
        w2b = sb("w2b", [DM, C])
        dw1 = sb("dw1", [P, CT, DD])
        dw2 = sb("dw2", [DD, C])
        sel = {n: sb("s_" + n, [P, SELW[n]]) for n in SELS}
        eps = sb("eps", [P, 1])
        spare = sb("spare", [P, 1])
        x_in = sb("x_in", [P, GB, C])
        x_res = sb("x_res", [P, GB, C])
        st_rows = sb("st_rows", [P, C])
        st_cols = sb("st_cols", [P, CT, 2, GB])
        s0 = sb("s0", [P, GB, CT, S])
        stats = sb("stats", [P, GB, 6])
        mv = sb("mv", [P, GB, 2])
        lnv = sb("lnv", [P, GB])
        rstd = sb("rstd", [P, GB])
        xa = sb("xa", [P, CT, GB, P + 1])
        sx = sb("sx", [P, CT, T])
        xz = [sb(f"xz{i}", [P, CT, T]) for i in range(2)]
        th0 = sb("th0", [4 * DM, T])
        th1 = sb("th1", [DM, T])
        dl = sb("dl", [DD, T])
        ew = sb("ew", [P, 2, T])
        w_sh = sb("w_sh", [P, CT, GB, P])
        k_pad = sb("k_pad", [P, CT, GB, P + 1])
        v_pad = sb("v_pad", [P, CT, GB, P + 1])
        r_sb = sb("r_sb", [P, CT, GB, P])
        g_sb = sb("g_sb", [P, CT, T])
        xn = g_sb[:, :, :]
        states = sb("states", [P, RING, GB, P])
        mixt = states[:, :, :, :].rearrange("p r b l -> p r (b l)")
        rr = mixt
        prods = sb("prods", [P, RING, T])
        rkf = sb("rkf", [P, GB, P])
        bon = sb("bon", [P, GB, P])
        y_sb = sb("y_sb", [P, T])
        ysq = sb("ysq", [P, T])
        lnr = ew[:, 0, :]
        rs = sb("rs", [P, T])
        z_sb = ysq
        yg = xz[1]
        x1 = x_res
        relu = ew
        kk = sx
        xk2, xr2 = xz
        bank = [ctx.enter_context(nc.psum_tensor(f"gen{i}", [P, T], F32)) for i in range(BANKS)]
        vb = [ctx.enter_context(nc.psum_tensor(f"vb{i}", [P, GB, P], F32)) for i in range(RING)]
        y_ps = ctx.enter_context(nc.psum_tensor("y_ps", [P, T], F32))

        const_in, x_landed, st_landed, s0_landed, res_landed, stored = (
            sem(n) for n in ("const_in", "x_landed", "st_landed", "s0_landed", "res_landed", "stored"))
        vec_in = sem("vec_in")
        preset = sem("preset")
        filled = sem("filled")
        act_drained = sem("act_drained")
        dve_drained = sem("dve_drained")
        stat = sem("stat")
        lnv_done = sem("lnv_done")
        rstd_done = sem("rstd_done")
        normed = sem("normed")
        shifted = sem("shifted")
        mixed_x = sem("mixed_x")
        mixed = sem("mixed")
        edge = sem("edge")
        decay_ready = sem("decay_ready")
        bcast, s0_put, kv, scanned, prodded, summed = (
            sem(n) for n in ("bcast", "s0_put", "kv", "scanned", "prodded", "summed"))
        bonus_in = sem("bonus_in")
        y_done = sem("y_done")
        squared = sem("squared")
        rs_ready = sem("rs_ready")
        yg_ready = sem("yg_ready")
        shifted2 = sem("shifted2")
        mixed2 = sem("mixed2")
        key_ready = sem("key_ready")
        gated = sem("gated")
        block = ctx.enter_context(nc.Block())

        def v_(name, c):
            return vec[:, VECS.index(name), c:c + 1]

        def at(g, count, n):
            return g * count + n

        def reuse(g, count, n, depth):
            return g * count + max(n + 1 - depth, 0)

        def fill_value(g, name):
            return at(g, len(uses), order[name] + 1)

        def wait_if(eng, s, value):
            if not (isinstance(value, int) and value <= 0):
                eng.wait_ge(s, value)

        def wait_drained(eng, g, name):
            s, w = (act_drained, "act") if who[name] == "act" else (dve_drained, "dve")
            eng.wait_ge(s, at(g, per[w], rank[name] + 1))

        def gbank(name):
            return bank[order[name] % BANKS]

        shifted_view = [xa[:, c, :, 0:P] for c in range(CT)]
        token_view = [xa[:, c, :, 1:P + 1] for c in range(CT)]

        def b3(ap):
            return ap.rearrange("p (b l) -> p b l", b=GB)

        @block.sync
        def _(sp):
            n_const = [0]

            def const(dst, src):
                sp.dma_start(dst, src).then_inc(const_in, 16)
                n_const[0] += 1

            def load(g, first=False):
                if first:
                    sp.wait_ge(preset, 5)
                sp.dma_start(x_in[:, :, :], x[bass.ds(g * GB, GB)].rearrange("b l c -> l b c")).then_inc(x_landed, 16)
                for j in range(2):
                    sp.dma_start(st_rows[j * GB:(j + 1) * GB, :],
                                 ctx_in[bass.ds(g * GB, GB), j, :]).then_inc(st_landed, 16)

            def load_late(g):
                wait_if(sp, s0_put, at(g, STEPS, 0))
                for b in range(GB):
                    sp.dma_start(s0[:, b, :, :], ctx_in[bass.ds(g * GB + b, 1), 2:2 + S, :].rearrange(
                        "b (ct hp) (hl s t) -> (b hp hl s) ct t", ct=CT, hl=2, t=S)).then_inc(s0_landed, 16)
                wait_if(sp, stored, at(g, 16 * GB, 0))
                sp.dma_start(x_res[:, :, :], x[bass.ds(g * GB, GB)].rearrange("b l c -> l b c")).then_inc(res_landed, 16)

            def store(g):
                for b in range(GB):
                    sp.wait_ge(gated, at(g, GB, b + 1))
                    sp.dma_start(out[bass.ds(g * GB + b, 1)].rearrange("b l c -> (b l) c"),
                                 x1[:, b, :]).then_inc(stored, 16)

            load(0, True)
            const(sel["ident"][:, :], sels["ident"])
            sp.dma_start(vec[:, :, :], vecs).then_inc(vec_in, 16)
            const(w1[:, :, :], maa_w1)
            const(w2a[:, :], maa_w2[0:4 * DM, :])
            const(w2b[:, :], maa_w2[4 * DM:5 * DM, :])
            const(dw1[:, :, :], decay_w1)
            const(dw2[:, :], decay_w2)
            for n in SELS[1:]:
                const(sel[n][:, :], sels[n])
            for n in MATS:
                const(mat[n][:, :, :], mats[n])
            load_late(0)

            def after(g, last):
                if not last:
                    sp.wait_ge(normed, at(g, 2 * GB, GB))
                    wait_drained(sp, g, "state")
                    load(g + 1)
                store(g)
                if not last:
                    load_late(g + 1)
            after(0, False)
            with sp.Fori(1, NG - 1) as g:
                after(g, False)
            after(NG - 1, True)
            sp.wait_ge(stored, 16 * GB * NG)

        @block.tensor
        def _(pe):
            N_CONST = 6 + len(SELS) - 1 + len(MATS)
            pe.wait_ge(const_in, 16 * N_CONST)

            def claim(g, name):
                n = order[name]
                if n >= BANKS:
                    wait_drained(pe, g, uses[n - BANKS][0])

            def product(name, pairs, rows=P):
                dst = gbank(name)[0:rows, :]
                for n, (lhsT, rhs) in enumerate(pairs):
                    ins = pe.matmul(dst, lhsT, rhs, start=(n == 0), stop=(n == len(pairs) - 1))
                ins.then_inc(filled, 1)

            def turn(g, name, srcs):
                claim(g, name)
                for n, src in enumerate(srcs):
                    ins = pe.transpose(gbank(name)[:, n * P:(n + 1) * P], src, sel["ident"][:, :])
                ins.then_inc(filled, 1)

            def mix(g, f):
                for c in range(CT):
                    claim(g, f"mix{f}_{c}")
                    cs = slice(c * P, (c + 1) * P)
                    if f < 4:
                        q = slice(DM * f, DM * (f + 1))
                        product(f"mix{f}_{c}", [(w2a[q, cs], th0[q, :])])
                    else:
                        product(f"mix{f}_{c}", [(w2b[:, cs], th1[:, :])])

            def proj(g, f, name):
                src = xz[f % 2]
                for c in range(CT):
                    claim(g, f"proj{f}_{c}")
                    if c == 0:
                        pe.wait_ge(mixed, at(g, NF * CT, CT * (f + 1)))
                    product(f"proj{f}_{c}", [(mat[name][:, k, c * P:(c + 1) * P], src[:, k, :]) for k in range(CT)])

            def scan_bcast(g, m):
                c, i, q = m // S, m % S // 4, m % 4
                if m % S == 0:
                    wait_drained(pe, g, f"proj2_{c}")
                wait_if(pe, scanned, reuse(g, STEPS, m, RING))
                pe.matmul(vb[q][:, :, :], sel["spread"][32 * q:32 * q + 32, i * P:(i + 1) * P],
                          v_pad[32 * q:32 * q + 32, c, :, 0:P], start=True, stop=True).then_inc(bcast, 1)

            def scan_sum(g, m):
                c, i, q = m // S, m % S // 4, m % 4
                if m % S == 0:
                    wait_if(pe, y_done, at(g, CT, c))
                pe.wait_ge(prodded, at(g, STEPS, m + 1))
                pe.matmul(y_ps[32 * q:32 * q + 32, :], sel["gather"][:, 32 * i:32 * i + 32],
                          prods[:, m % RING, :], start=(i == 0), stop=(i == 3)).then_inc(summed, 1)

            def group(g):
                wait_if(pe, act_drained, at(g, per["act"], 0))
                wait_if(pe, dve_drained, at(g, per["dve"], 0))
                pe.wait_ge(st_landed, at(g, 32, 32))
                turn(g, "state", [st_rows[:, c * P:(c + 1) * P] for c in range(CT)])
                pe.wait_ge(normed, at(g, 2 * GB, GB))
                for c in range(CT):
                    turn(g, f"tr1_{c}", [xn[:, b, c * P:(c + 1) * P] for b in range(GB)])
                pe.wait_ge(mixed_x, at(g, CT, CT))
                claim(g, "lora0")
                product("lora0", [(w1[:, k, 0:P], xz[0][:, k, :]) for k in range(CT)])
                claim(g, "lora1")
                product("lora1", [(w1[:, k, P:P + DM], xz[0][:, k, :]) for k in range(CT)], DM)
                wait_drained(pe, g, "lora1")
                mix(g, 0)
                mix(g, 1)
                claim(g, "decay_in")
                pe.wait_ge(mixed, at(g, NF * CT, CT))
                product("decay_in", [(dw1[:, k, :], xz[0][:, k, :]) for k in range(CT)], DD)
                wait_drained(pe, g, "decay_in")
                for c in range(CT):
                    claim(g, f"proj0_{c}")
                    product(f"proj0_{c}", [(dw2[:, c * P:(c + 1) * P], dl[:, :])])
                mix(g, 2)
                proj(g, 1, "Wk")
                mix(g, 3)
                proj(g, 2, "Wv")
                mix(g, 4)
                proj(g, 3, "Wr")
                proj(g, 4, "Wg")
                for c in range(CT):
                    claim(g, f"bonus_{c}")
                    pe.wait_ge(bonus_in, at(g, CT, c + 1))
                    product(f"bonus_{c}", [(sel["headsum"][:, :], rkf[:, :, :])])
                    for j in range(S + RING - 1):
                        if j < S:
                            scan_bcast(g, c * S + j)
                        if j >= RING - 1:
                            scan_sum(g, c * S + j - RING + 1)
                    claim(g, f"center_{c}")
                    pe.wait_ge(y_done, at(g, CT, c + 1))
                    product(f"center_{c}", [(sel["center"][:, :], y_sb[:, :])])
                    claim(g, f"var_{c}")
                    pe.wait_ge(squared, at(g, CT, c + 1))
                    product(f"var_{c}", [(sel["headmean"][:, :], ysq[:, :])])
                pe.wait_ge(yg_ready, at(g, CT, CT))
                for b in range(GB):
                    claim(g, f"wo_{b}")
                    product(f"wo_{b}", [(yg[:, k, b * P:(b + 1) * P], mat["Wo"][:, k, :]) for k in range(CT)])
                pe.wait_ge(normed, at(g, 2 * GB, 2 * GB))
                for c in range(CT):
                    turn(g, f"tr2_{c}", [xn[:, b, c * P:(c + 1) * P] for b in range(GB)])
                pe.wait_ge(mixed2, at(g, 2 * CT, 2 * CT))
                for c in range(CT):
                    claim(g, f"key_{c}")
                    product(f"key_{c}", [(mat["fWk"][:, k, c * P:(c + 1) * P], xk2[:, k, :]) for k in range(CT)])
                for b in range(GB):
                    claim(g, f"recept_{b}")
                    product(f"recept_{b}", [(xr2[:, k, b * P:(b + 1) * P], mat["fWr"][:, k, :]) for k in range(CT)])
                    if b == 0:
                        pe.wait_ge(key_ready, at(g, CT, CT))
                    claim(g, f"value_{b}")
                    product(f"value_{b}", [(kk[:, k, b * P:(b + 1) * P], mat["fWv"][:, k, :]) for k in range(CT)])
            group(0)
            with pe.Fori(1, NG) as g:
                group(g)

        @block.scalar
        def _(act):
            act.wait_ge(vec_in, 16)
            act.wait_ge(preset, 5)

            def full(g, name):
                act.wait_ge(filled, fill_value(g, name))

            def layernorm_rstd(g, n):
                act.wait_ge(stat, at(g, 4 * GB, 2 * GB * (n + 1)))
                act.activation(lnv[:, :], mv[:, :, 1], ACT.Ln, bias=eps[:, :]).then_inc(lnv_done, 1)
                act.wait_ge(lnv_done, at(g, 2, n + 1))
                act.activation(rstd[:, :], lnv[:, :], ACT.Exp, scale=-0.5).then_inc(rstd_done, 1)

            def channel_major(g, n, w, b, c):
                full(g, f"tr{n}_{c}")
                act.activation(token_view[c], b3(gbank(f"tr{n}_{c}")[:, :]), ACT.Identity, bias=v_(b, c),
                               scale=v_(w, c)).then_inc(act_drained, 1)

            def group(g):
                full(g, "state")
                act.activation(st_cols[:, :, :, :].rearrange("p c j b -> p c (j b)"),
                               gbank("state")[:, :].rearrange("p (c n) -> p c n", c=CT)[:, :, 0:2 * GB], ACT.Copy).then_inc(act_drained, 1)
                wait_drained(act, g, "state")
                wait_if(act, shifted2, at(g, CT, 0))
                wait_if(act, mixed2, at(g, 2 * CT, 0))
                act.activation(xa[:, :, :, 0], st_cols[:, :, 1, :], ACT.Copy).then_inc(edge, 1)
                layernorm_rstd(g, 0)
                for c in range(CT):
                    channel_major(g, 1, "ln1_w", "ln1_b", c)
                full(g, "lora0")
                act.activation(th0[:, :], gbank("lora0")[:, :], ACT.Tanh).then_inc(act_drained, 1)
                full(g, "lora1")
                act.activation(th1[:, :], gbank("lora1")[0:DM, :], ACT.Tanh).then_inc(act_drained, 1)
                full(g, "decay_in")
                act.activation(dl[:, :], gbank("decay_in")[0:DD, :], ACT.Tanh).then_inc(act_drained, 1)
                for c in range(CT):
                    name = f"proj0_{c}"
                    full(g, name)
                    wait_if(act, decay_ready, at(g, CT, c - 1) if c > 1 else at(g, CT, 0))
                    act.activation(ew[:, c % 2, :], gbank(name)[:, :], ACT.Exp,
                                   bias=v_("time_decay", c)).then_inc(act_drained, 1)
                    wait_drained(act, g, name)
                    act.activation(w_sh[:, c, :, 1:P], b3(ew[:, c % 2, :])[:, :, 0:P - 1], ACT.Exp,
                                   scale=-1.0).then_inc(decay_ready, 1)
                for f, dst in ((1, k_pad), (2, v_pad)):
                    for c in range(CT):
                        full(g, f"proj{f}_{c}")
                        act.activation(dst[:, c, :, 1:P + 1], b3(gbank(f"proj{f}_{c}")[:, :]),
                                       ACT.Copy).then_inc(act_drained, 1)
                for c in range(CT):
                    full(g, f"proj3_{c}")
                    act.activation(r_sb[:, c, :, :], b3(gbank(f"proj3_{c}")[:, :]), ACT.Copy).then_inc(act_drained, 1)
                for c in range(CT):
                    full(g, f"proj4_{c}")
                    act.activation(g_sb[:, c, :], gbank(f"proj4_{c}")[:, :], ACT.Silu).then_inc(act_drained, 1)
                act.wait_ge(s0_landed, at(g, 16 * GB, 16 * GB))
                for c in range(CT):
                    for j in range(S):
                        m, i, q = c * S + j, j // 4, j % 4
                        act.wait_ge(bcast, at(g, STEPS, m + 1))
                        act.activation(vb[q][:, :, 0], s0[:, :, c, 4 * q + i], ACT.Copy).then_inc(s0_put, 1)
                    full(g, f"center_{c}")
                    act.activation(ysq[:, :], gbank(f"center_{c}")[:, :], ACT.Square).then_inc(squared, 1)
                    full(g, f"var_{c}")
                    act.activation(lnr, gbank(f"var_{c}")[:, :], ACT.Ln, bias=eps[:, :]).then_inc(act_drained, 1)
                    wait_drained(act, g, f"var_{c}")
                    act.activation(rs[:, :], lnr, ACT.Exp, scale=-0.5).then_inc(rs_ready, 1)
                act.activation(xa[:, :, :, 0], st_cols[:, :, 0, :], ACT.Copy).then_inc(edge, 1)
                layernorm_rstd(g, 1)
                for c in range(CT):
                    channel_major(g, 2, "ln2_w", "ln2_b", c)
                for c in range(CT):
                    full(g, f"key_{c}")
                    wait_if(act, key_ready, at(g, CT, c - 1) if c > 1 else at(g, CT, 0))
                    act.activation(relu[:, c % 2, :], gbank(f"key_{c}")[:, :], ACT.Relu).then_inc(act_drained, 1)
                    wait_drained(act, g, f"key_{c}")
                    act.activation(kk[:, c, :], relu[:, c % 2, :], ACT.Square).then_inc(key_ready, 1)
                for b in range(GB):
                    full(g, f"recept_{b}")
                    if b >= 2:
                        act.wait_ge(gated, at(g, GB, b - 1))
                    else:
                        wait_if(act, gated, at(g, GB, 0))
                    act.activation(rr[:, b % 2, :], gbank(f"recept_{b}")[:, :], ACT.Sigmoid).then_inc(act_drained, 1)
            group(0)
            with act.Fori(1, NG) as g:
                group(g)

        @block.vector
        def _(dve):
            dve.memset(st_rows[:, :], 0.0).then_inc(preset, 1)
            dve.memset(eps[:, :], EPS).then_inc(preset, 1)
            dve.memset(w_sh[:, :, :, 0], 0.0).then_inc(preset, 1)
            dve.memset(k_pad[:, :, :, 0], 1.0).then_inc(preset, 1)
            dve.memset(v_pad[:, :, :, 0], 0.0).then_inc(preset, 1)
            dve.wait_ge(preset, 5)
            dve.wait_ge(vec_in, 16)

            def layernorm(g, n, src):
                for b in range(GB):
                    dve.bn_stats(stats[:, b, :], src(b)).then_inc(stat, 1)
                dve.wait_ge(stat, at(g, 4 * GB, 2 * GB * n + GB))
                dve.memset(spare[:, :], 0.0)
                for b in range(GB):
                    dve.bn_aggr(mv[:, b, :], stats[:, b, :]).then_inc(stat, 1)
                dve.wait_ge(stat, at(g, 4 * GB, 2 * GB * (n + 1)))
                dve.wait_ge(rstd_done, at(g, 2, n + 1))

            def group(g):
                dve.wait_ge(x_landed, at(g, 16, 16))
                layernorm(g, 0, lambda b: x_in[:, b, :])
                for b in range(GB):
                    dve.tensor_scalar(xn[:, b, :], x_in[:, b, :], mv[:, b, 0:1], rstd[:, b:b + 1],
                                      ALU.subtract, ALU.mult).then_inc(normed, 1)
                dve.wait_ge(edge, at(g, 2, 1))
                wait_if(dve, filled, at(g, len(uses), 0))
                for c in range(CT):
                    wait_drained(dve, g, f"tr1_{c}")
                    dve.tensor_tensor(b3(sx[:, c, :]), shifted_view[c], token_view[c], ALU.subtract).then_inc(shifted, 1)
                for c in range(CT):
                    dve.wait_ge(shifted, at(g, CT, c + 1))
                    dve.scalar_tensor_tensor(out=b3(xz[0][:, c, :]), in0=b3(sx[:, c, :]), scalar=v_("maa_x", c),
                                             in1=token_view[c], op0=ALU.mult, op1=ALU.add).then_inc(mixed_x, 1)
                for f, name in enumerate(("maa_w", "maa_k", "maa_v", "maa_r", "maa_g")):
                    for c in range(CT):
                        n = f * CT + c
                        dve.wait_ge(filled, fill_value(g, f"mix{f}_{c}"))
                        wait_if(dve, mixed, reuse(g, NF * CT, n, RING))
                        dve.scalar_tensor_tensor(out=mixt[:, n % RING, :], in0=gbank(f"mix{f}_{c}")[:, :],
                                                 scalar=v_(name, c), in1=sx[:, c, :], op0=ALU.add,
                                                 op1=ALU.mult).then_inc(dve_drained, 1)
                for c in range(CT):
                    wait_drained(dve, g, f"proj3_{c}")
                    dve.scalar_tensor_tensor(out=rkf[:, :, :], in0=r_sb[:, c, :, :], scalar=v_("faaaa", c),
                                             in1=k_pad[:, c, :, 1:P + 1], op0=ALU.mult, op1=ALU.mult).then_inc(bonus_in, 1)
                    dve.wait_ge(decay_ready, at(g, CT, c + 1))
                    dve.wait_ge(filled, fill_value(g, f"bonus_{c}"))
                    dve.tensor_tensor(bon[:, :, :], b3(gbank(f"bonus_{c}")[:, :]), v_pad[:, c, :, 1:P + 1],
                                      ALU.mult).then_inc(dve_drained, 1)
                    for j in range(S + 1):
                        m = c * S + j
                        if j < S:
                            dve.wait_ge(s0_put, at(g, STEPS, m + 1))
                            dve.tensor_tensor(vb[m % RING][:, :, :], vb[m % RING][:, :, :], k_pad[:, c, :, 0:P],
                                              ALU.mult).then_inc(kv, 1)
                        if j >= 1:
                            m -= 1
                            dve.wait_ge(kv, at(g, STEPS, m + 1))
                            wait_if(dve, prodded, reuse(g, STEPS, m, RING))
                            dve.tensor_tensor_scan(states[:, m % RING, :, :].rearrange("p b l -> p (b l)"),
                                                   w_sh[:, c, :, :].rearrange("p b l -> p (b l)"),
                                                   vb[m % RING][:, :, :].rearrange("p b l -> p (b l)"),
                                                   0.0, ALU.mult, ALU.add).then_inc(scanned, 1)
                    dve.wait_ge(summed, at(g, STEPS, (c + 1) * S))
                    wait_drained(dve, g, f"bonus_{c}")
                    dve.tensor_tensor(y_sb[:, :], y_ps[:, :], bon[:, :, :].rearrange("p b l -> p (b l)"),
                                      ALU.add).then_inc(y_done, 1)
                    dve.wait_ge(rs_ready, at(g, CT, c + 1))
                    dve.scalar_tensor_tensor(out=z_sb[:, :], in0=gbank(f"center_{c}")[:, :], scalar=v_("gn_w", c),
                                             in1=rs[:, :], op0=ALU.mult, op1=ALU.mult).then_inc(dve_drained, 1)
                    wait_drained(dve, g, f"center_{c}")
                    wait_drained(dve, g, f"proj4_{c}")
                    dve.scalar_tensor_tensor(out=yg[:, c, :], in0=z_sb[:, :], scalar=v_("gn_b", c),
                                             in1=g_sb[:, c, :], op0=ALU.add, op1=ALU.mult).then_inc(yg_ready, 1)

                dve.wait_ge(res_landed, at(g, 16, 16))

                def residual(b):
                    dve.wait_ge(filled, fill_value(g, f"wo_{b}"))
                    dve.tensor_tensor(x1[:, b, :], gbank(f"wo_{b}")[:, :], x_res[:, b, :], ALU.add).then_inc(dve_drained, 1)
                    wait_drained(dve, g, f"wo_{b}")
                    return x1[:, b, :]
                layernorm(g, 1, residual)
                for b in range(GB):
                    dve.tensor_scalar(xn[:, b, :], x1[:, b, :], mv[:, b, 0:1], rstd[:, b:b + 1],
                                      ALU.subtract, ALU.mult).then_inc(normed, 1)
                dve.wait_ge(edge, at(g, 2, 2))
                for c in range(CT):
                    wait_drained(dve, g, f"tr2_{c}")
                    dve.tensor_tensor(b3(kk[:, c, :]), shifted_view[c], token_view[c],
                                      ALU.subtract).then_inc(shifted2, 1)
                for c in range(CT):
                    dve.wait_ge(shifted2, at(g, CT, c + 1))
                    for dst, name in ((xk2, "fmaa_k"), (xr2, "fmaa_r")):
                        dve.scalar_tensor_tensor(out=b3(dst[:, c, :]), in0=b3(kk[:, c, :]), scalar=v_(name, c),
                                                 in1=token_view[c], op0=ALU.mult, op1=ALU.add).then_inc(mixed2, 1)
                for b in range(GB):
                    dve.wait_ge(filled, fill_value(g, f"value_{b}"))
                    wait_drained(dve, g, f"recept_{b}")
                    dve.tensor_tensor(rr[:, b % 2, :], gbank(f"value_{b}")[:, :], rr[:, b % 2, :],
                                      ALU.mult).then_inc(dve_drained, 1)
                    wait_drained(dve, g, f"value_{b}")
                    dve.tensor_tensor(x1[:, b, :], rr[:, b % 2, :], x1[:, b, :], ALU.add).then_inc(gated, 1)
            group(0)
            with dve.Fori(1, NG) as g:
                group(g)

        @block.gpsimd
        def _(pool):
            def group(g):
                for f in range(NF):
                    for c in range(CT):
                        n = f * CT + c
                        pool.wait_ge(dve_drained, at(g, per["dve"], rank[f"mix{f}_{c}"] + 1))
                        if c == 0 and f == 0:
                            wait_drained(pool, g, "lora1")
                        if c == 0 and f == 1:
                            wait_if(pool, filled, at(g, len(uses), 0))
                        if c == 0 and f >= 2:
                            last = "decay_in" if f == 2 else f"proj{f - 2}_{CT - 1}"
                            pool.wait_ge(filled, fill_value(g, last))
                        pool.tensor_tensor(b3(xz[f % 2][:, c, :]), b3(mixt[:, n % RING, :]), token_view[c],
                                           ALU.add).then_inc(mixed, 1)
                for m in range(STEPS):
                    if m % S == 0:
                        wait_drained(pool, g, f"proj3_{m // S}")
                    pool.wait_ge(scanned, at(g, STEPS, m + 1))
                    wait_if(pool, summed, reuse(g, STEPS, m, RING))
                    pool.tensor_tensor(b3(prods[:, m % RING, :]), states[:, m % RING, :, :],
                                       r_sb[:, m // S, :, :], ALU.mult).then_inc(prodded, 1)
            group(0)
            with pool.Fori(1, NG) as g:
                group(g)


def kernel(**inputs):
    import numpy as np
    import concourse.bacc as bacc
    from concourse.bass_utils import run_bass_kernel_spmd

    def arr(name):
        return np.asarray(inputs["L0_xattn_" + name])

    def perm(a, axis):
        a = np.moveaxis(a, axis, 0)
        a = a.reshape(CT, HT, S, *a.shape[1:]).swapaxes(1, 2).reshape(a.shape)
        return np.moveaxis(a, 0, axis)

    def tiles(a):
        return np.ascontiguousarray(a.reshape(CT, P, -1).transpose(1, 0, 2))

    arrays = {"x": np.ascontiguousarray(inputs["x"]), "ctx_in": np.ascontiguousarray(inputs["ctx_2048"])}
    cols = [perm(arr(n), 0) if n in ("gn_w", "gn_b") else arr(n).reshape(C) for n in VECS]
    arrays["vecs"] = np.ascontiguousarray(np.stack(cols).reshape(len(VECS), CT, P).transpose(2, 0, 1))
    for n in MATS:
        w = arr(n).T
        if n in ("Wv", "Wg"):
            w = perm(w, 1)
        if n == "Wo":
            w = perm(w, 0)
        arrays["m_" + n] = tiles(w)
    arrays["maa_w1"] = tiles(arr("maa_w1"))
    arrays["maa_w2"] = np.ascontiguousarray(arr("maa_w2").reshape(NF * DM, C))
    arrays["decay_w1"] = tiles(arr("decay_w1"))
    arrays["decay_w2"] = np.ascontiguousarray(arr("decay_w2"))

    head_n, s_n = np.arange(P) // S, np.arange(P) % S
    t_y, head_y = np.arange(P) // HT, np.arange(P) % HT
    same_ny = (head_n[:, None] == head_y[None, :])
    same_yy = (head_y[:, None] == head_y[None, :])
    spread = np.stack([(t_y % 4 == i)[:, None] & same_ny.T for i in range(4)], 1)
    local = np.arange(32)
    gather = np.stack([(local // HT == i)[None, :] & (head_n[:, None] == (local % HT)[None, :]) for i in range(4)], 1)
    consts = {"ident": np.eye(P), "spread": spread.reshape(P, 4 * P), "gather": gather.reshape(P, 128),
              "headsum": same_ny, "center": np.eye(P) - same_yy / S, "headmean": same_yy / S}
    for n in SELS:
        arrays["s_" + n] = np.ascontiguousarray(consts[n].astype(np.float32))

    nc = bacc.Bacc("TRN2", target_bir_lowering=False, num_devices=1)
    ap = {n: nc.dram_tensor("in_" + n, a.shape, F32, kind="ExternalInput").ap() for n, a in arrays.items()}
    shape = inputs["x"].shape
    out = nc.dram_tensor("out_y", shape, F32, kind="ExternalOutput").ap()
    rwkv_kernel(nc, ap["x"], ap["ctx_in"], ap["vecs"], {n: ap["m_" + n] for n in MATS}, ap["maa_w1"], ap["maa_w2"],
                ap["decay_w1"], ap["decay_w2"], {n: ap["s_" + n] for n in SELS}, out)
    r = run_bass_kernel_spmd(nc, [{"in_" + n: a for n, a in arrays.items()}], core_ids=[0])
    return r.results[0]["out_y"]
```

```python
from contextlib import ExitStack

import concourse.bass as bass
from concourse import mybir

F32 = mybir.dt.float32
F32R = mybir.dt.float32r
ALU = mybir.AluOpType
ACT = mybir.ActivationFunctionType

P = 128
GB = 4
T = GB * P
CT = 4
C = CT * P
S = 16
HT = P // S
DM, DD = 32, 64
EPS = 1e-5
NF = 5
BANKS = 3
STEPS = CT * S
RING = 4
PRING = 3
LAG = 4

VECS = ["ln1_w", "ln1_b", "ln2_w", "ln2_b", "maa_x", "maa_w", "maa_k", "maa_v", "maa_r", "maa_g",
        "time_decay", "faaaa", "gn_w", "gn_b", "fmaa_k", "fmaa_r"]
MATS = ["Wr", "Wk", "Wv", "Wg", "Wo", "fWk", "fWr", "fWv"]
SELS = ["ident", "gather", "headsum", "center", "headmean"]


FRONT = ["state"] + [f"tr1_{c}" for c in range(CT)]


def beside_scan(c):
    nxt = c + 1 < CT
    v, k, r = ((f"proj{f}_{c + 1}" if nxt else None) for f in (2, 1, 3))
    g = f"proj4_{c - 1}" if c >= 1 else None
    return [v, g, k, r if nxt else "proj4_3"]


def general_uses():
    uses = ["lora0", "lora1"] + [f"mix{f}_{c}" for f in (0, 1) for c in range(CT)] + ["decay_in"]
    uses += [f"mix{f}_{c}" for f in (2, 3) for c in range(CT)] + [f"proj0_{c}" for c in range(CT)]
    uses += [f"mix4_{c}" for c in range(CT)] + ["proj2_0", "proj1_0", "proj3_0"]
    for c in range(CT):
        for quarter, name in enumerate(beside_scan(c)):
            uses += [name] if name else []
            if quarter == 0:
                uses.append(f"bonus_{c}")
            if quarter == 1 and c >= 1:
                uses.append(f"center_{c - 1}")
            if quarter == 2 and c >= 1:
                uses.append(f"var_{c - 1}")
    uses += ["center_3", "var_3"] + [f"wo_{b}" for b in range(GB)]
    uses += [f"tr2_{c}" for c in range(CT)] + [f"key_{c}" for c in range(CT)] + FRONT
    for b in range(GB):
        uses += [f"recept_{b}", f"value_{b}"]
    return [(u, "dve" if u[:3] in ("mix", "bon", "wo_", "val") else "act") for u in uses]


def rwkv_kernel(nc, x, ctx_in, vecs, mats, maa_w1, maa_w2, decay_w1, decay_w2, sels, out):
    NB = x.shape[0]
    NG = NB // GB
    uses = general_uses()
    names = [u for u, _ in uses]
    who = dict(uses)
    order = {u: n for n, u in enumerate(names)}
    rank = {u: sum(who[o] == who[u] for o in names[:order[u]]) for u in names}
    per = {w: sum(who[u] == w for u in names) for w in ("act", "dve")}

    with ExitStack() as ctx:
        def sb(name, shape, dt=F32):
            return ctx.enter_context(nc.sbuf_tensor(name, shape, dt))

        def sem(name):
            return ctx.enter_context(nc.semaphore(name))

        vec = sb("vec", [P, len(VECS), CT])
        mat = {n: sb("m_" + n, [P, CT, C]) for n in MATS}
        w1 = sb("w1", [P, CT, NF * DM])
        w2 = sb("w2", [P, NF, C])
        dw1 = sb("dw1", [P, CT, DD])
        dw2 = sb("dw2", [P, C])
        sel = {n: sb("s_" + n, [P, P]) for n in SELS}
        spread = sb("spread", [P, P, S], F32R)
        eps = sb("eps", [P, 1])
        spare = sb("spare", [P, 1])
        x1 = sb("x1", [P, GB, C])
        st_rows = sb("st_rows", [P, C])
        st_cols = sb("st_cols", [P, CT, 2, GB])
        s0 = sb("s0", [P, GB, CT, S])
        stats = sb("stats", [P, 2, GB, 6])
        mv = sb("mv", [P, 2, GB, 2])
        lnv = sb("lnv", [P, 2, GB])
        rstd = sb("rstd", [P, 2, GB])
        xa = sb("xa", [P, CT, GB, P + 1])
        sx = sb("sx", [P, CT, T])
        buf = [sb(f"buf{i}", [P, CT, T]) for i in range(4)]
        xn = buf[0]
        xxx = buf[1]
        mixed_in = [buf[0], buf[1], buf[2], buf[3], buf[0]]
        xk2, xr2 = buf[2], buf[3]
        th0 = sb("th0", [P, T])
        bon = sb("bon", [P, T])
        th1 = bon
        rs = sb("rs", [P, T])
        dl = rs
        w_sh = sb("w_sh", [P, CT, GB, P])
        x_in = w_sh[:, :, :, :].rearrange("p c b l -> p c (b l)")
        k_pad = sb("k_pad", [P, 2, GB, P + 1])
        v_pad = sb("v_pad", [P, 2, GB, P + 1])
        v_parts = sb("v_parts", [P, 2, 2, T], F32R)
        r_sb = sb("r_sb", [P, CT, GB, P])
        kk = r_sb[:, :, :, :].rearrange("p c b l -> p c (b l)")
        yg = sb("yg", [P, CT, T])
        states = sb("states", [P, RING, GB, P])
        mixt = states[:, :, :, :].rearrange("p r b l -> p r (b l)")
        rr = mixt
        prods = sx[:, 0:PRING, :]
        rkf = sx[:, PRING, :]
        ysq = rkf
        z_sb = rkf
        y_sb = sb("y_sb", [P, T])
        bank = [ctx.enter_context(nc.psum_tensor(f"gen{i}", [P, T], F32)) for i in range(BANKS)]
        vb = [ctx.enter_context(nc.psum_tensor(f"vb{i}", [P, GB, P], F32)) for i in range(RING)]
        y_ps = ctx.enter_context(nc.psum_tensor("y_ps", [P, T], F32))

        vec_in = sem("vec_in")
        ident_in = sem("ident_in")
        w_in = [sem(f"w_in{i}") for i in range(4)]
        x_landed, st_landed, s0_landed, res_landed, stored = (
            sem(n) for n in ("x_landed", "st_landed", "s0_landed", "res_landed", "stored"))
        preset = sem("preset")
        zeroed = sem("zeroed")
        spread_ready = sem("spread_ready")
        filled = sem("filled")
        drained = {"act": sem("act_drained"),
                   "dve": sem("dve_drained")}
        stat, lnv_done, rstd_done, normed, edge = (
            [sem(f"{n}{i}") for i in (1, 2)] for n in ("stat", "lnv_done", "rstd_done", "normed", "edge"))
        shifted = sem("shifted")
        mixed_x = sem("mixed_x")
        mixed = [sem("mixed_pool"), sem("mixed_dve")]
        doubled = sem("doubled")
        v_high, v_low = sem("v_high"), sem("v_low")
        bcast, s0_put, kv, scanned, prodded, summed = (
            sem(n) for n in ("bcast", "s0_put", "kv", "scanned", "prodded", "summed"))
        bonus_in = sem("bonus_in")
        y_done = sem("y_done")
        squared = sem("squared")
        rooted = sem("rooted")
        z_done = sem("z_done")
        yg_ready = sem("yg_ready")
        shifted2 = sem("shifted2")
        xk2_ready, xr2_ready = sem("xk2_ready"), sem("xr2_ready")
        relu_done = sem("relu_done")
        gated = sem("gated")
        block = ctx.enter_context(nc.Block())

        def v_(name, c):
            return vec[:, VECS.index(name), c:c + 1]

        def at(g, count, n):
            return g * count + n

        def reuse(g, count, n, depth):
            return g * count + max(n + 1 - depth, 0)

        def wait_if(eng, s, value):
            if not (isinstance(value, int) and value <= 0):
                eng.wait_ge(s, value)

        def general_count(g, name, count, n, ahead):
            if name in FRONT:
                if isinstance(g, int) and g == 0:
                    return FRONT.index(name) + 1
                g = g - 1
            return g * count + ahead + n + 1

        def wait_filled(eng, g, name):
            eng.wait_ge(filled, general_count(g, name, len(names), order[name], len(FRONT)))

        def wait_drained(eng, g, name):
            w = who[name]
            ahead = len(FRONT) if w == "act" else 0
            eng.wait_ge(drained[w], general_count(g, name, per[w], rank[name], ahead))

        def gbank(name):
            return bank[order[name] % BANKS]

        shifted_view = [xa[:, c, :, 0:P] for c in range(CT)]
        token_view = [xa[:, c, :, 1:P + 1] for c in range(CT)]

        def b3(ap):
            return ap.rearrange("p (b l) -> p b l", b=GB)

        @block.sync
        def _(sp):
            def load(g):
                sp.dma_start(x_in, x[bass.ds(g * GB, GB)].rearrange("b l c -> l b c")).then_inc(x_landed, 16)
                for j in range(2):
                    sp.dma_start(st_rows[j * GB:(j + 1) * GB, :],
                                 ctx_in[bass.ds(g * GB, GB), j, :]).then_inc(st_landed, 16)

            def load_late(g):
                wait_if(sp, s0_put, at(g, STEPS, 0))
                for b in range(GB):
                    sp.dma_start(s0[:, b, :, :], ctx_in[bass.ds(g * GB + b, 1), 2:2 + S, :].rearrange(
                        "b (ct hp) (hl s t) -> (b hp hl s) ct t", ct=CT, hl=2, t=S)).then_inc(s0_landed, 16)
                wait_if(sp, stored, at(g, 16 * GB, 0))
                sp.dma_start(x1[:, :, :], x[bass.ds(g * GB, GB)].rearrange("b l c -> l b c")).then_inc(res_landed, 16)

            def store(g):
                for b in range(GB):
                    sp.wait_ge(gated, at(g, GB, b + 1))
                    sp.dma_start(out[bass.ds(g * GB + b, 1)].rearrange("b l c -> (b l) c"),
                                 x1[:, b, :]).then_inc(stored, 16)

            sp.wait_ge(preset, 1)
            load(0)
            sp.dma_start(sel["ident"][:, :], sels["ident"]).then_inc(ident_in, 16)
            sp.dma_start(vec[:, :, :], vecs).then_inc(vec_in, 16)
            for i, group in enumerate([
                    [(w1[:, :, :], maa_w1), (w2[:, :, :], maa_w2), (dw1[:, :, :], decay_w1), (dw2[:, :], decay_w2)],
                    [(mat[n][:, :, :], mats[n]) for n in ("Wv", "Wk", "Wr")],
                    [(sel[n][:, :], sels[n]) for n in SELS[1:]],
                    [(mat[n][:, :, :], mats[n]) for n in ("Wg", "Wo", "fWk", "fWr", "fWv")]]):
                for dst, src in group:
                    sp.dma_start(dst, src).then_inc(w_in[i], 16)
                if i == 1:
                    load_late(0)

            def after(g, last):
                nxt = g if last else g + 1
                sp.wait_ge(scanned, at(g, STEPS, STEPS))
                wait_drained(sp, g, "state")
                load(nxt)
                store(g)
                if not last:
                    load_late(g + 1)
            after(0, False)
            with sp.Fori(1, NG - 1) as g:
                after(g, False)
            after(NG - 1, True)
            sp.wait_ge(stored, 16 * GB * NG)

        @block.tensor
        def _(pe):
            def claim(g, name):
                n = order[name]
                if name in FRONT and isinstance(g, int) and g == 0:
                    if FRONT.index(name) >= BANKS:
                        wait_drained(pe, g, FRONT[FRONT.index(name) - BANKS])
                    return
                it = g - 1 if name in FRONT else g
                before = [m for m in range(n) if m % BANKS == n % BANKS]
                if before:
                    prev = names[before[-1]]
                else:
                    prev = [u for u in names if order[u] % BANKS == n % BANKS][-1]
                    if isinstance(it, int) and it == 0:
                        pe.wait_ge(drained["act"], len(FRONT))
                        return
                    it = it - 1
                wait_drained(pe, it + 1 if prev in FRONT else it, prev)

            def product(g, name, pairs, rows=P, ready=None):
                claim(g, name)
                for k, (lhsT, rhs) in enumerate(pairs):
                    if ready:
                        ready(k)
                    ins = pe.matmul(gbank(name)[0:rows, :], lhsT, rhs, start=(k == 0), stop=(k == len(pairs) - 1))
                ins.then_inc(filled, 1)

            def turn(g, name, srcs):
                claim(g, name)
                for n, src in enumerate(srcs):
                    ins = pe.transpose(gbank(name)[:, n * P:(n + 1) * P], src, sel["ident"][:, :])
                ins.then_inc(filled, 1)

            def mix(g, f):
                for c in range(CT):
                    product(g, f"mix{f}_{c}", [(w2[:, f, c * P:(c + 1) * P], (th0 if f < 4 else th1)[:, :])])

            def mixed_ready(g, f, k):
                pe.wait_ge(mixed[k % 2], at(g, NF * CT // 2, f * CT // 2 + k // 2 + 1))

            def proj_operands(name):
                f, c = int(name[4]), int(name[6])
                m = mat[{1: "Wk", 2: "Wv", 3: "Wr", 4: "Wg"}[f]]
                return [(m[:, k, c * P:(c + 1) * P], mixed_in[f][:, k, :]) for k in range(CT)]

            def front(g):
                pe.wait_ge(st_landed, at(g, 32, 32))
                turn(g, "state", [st_rows[:, c * P:(c + 1) * P] for c in range(CT)])
                pe.wait_ge(normed[0], at(g, GB, GB))
                for c in range(CT):
                    turn(g, f"tr1_{c}", [xn[:, b, c * P:(c + 1) * P] for b in range(GB)])

            def scan_bcast(g, m):
                c, j = m // S, m % S
                t = 4 * (j % 4) + j // 4
                if j == 0:
                    pe.wait_ge(v_high, at(g, CT, c + 1))
                    pe.wait_ge(v_low, at(g, CT, c + 1))
                wait_if(pe, scanned, reuse(g, STEPS, m, RING))
                pick = spread[:, t * HT:(t + 1) * HT, :].rearrange("p h s -> p (h s)")
                for part in range(2):
                    ins = pe.matmul(vb[m % RING][:, :, :], pick, b3(v_parts[:, c % 2, part, :]),
                                    start=(part == 0), stop=(part == 1))
                ins.then_inc(bcast, 1)

            def scan_sum(g, m):
                c, i, q = m // S, m % S // 4, m % 4
                if m % S == 0:
                    wait_if(pe, y_done, at(g, CT, c))
                pe.wait_ge(prodded, at(g, STEPS, m + 1))
                pe.matmul(y_ps[32 * q:32 * q + 32, :], sel["gather"][:, 32 * i:32 * i + 32],
                          prods[:, m % PRING, :], start=(i == 0), stop=(i == 3)).then_inc(summed, 1)

            def center(g, c):
                pe.wait_ge(y_done, at(g, CT, c + 1))
                product(g, f"center_{c}", [(sel["center"][:, :], y_sb[:, :])])

            def variance(g, c):
                pe.wait_ge(squared, at(g, CT, c + 1))
                product(g, f"var_{c}", [(sel["headmean"][:, :], ysq)])

            def group(g, first=False):
                product(g, "lora0", [(w1[:, k, 0:P], xxx[:, k, :]) for k in range(CT)],
                        ready=lambda k: pe.wait_ge(mixed_x, at(g, CT, k + 1)))
                product(g, "lora1", [(w1[:, k, P:P + DM], xxx[:, k, :]) for k in range(CT)], DM)
                wait_drained(pe, g, "lora0")
                mix(g, 0)
                mix(g, 1)
                product(g, "decay_in", [(dw1[:, k, :], mixed_in[0][:, k, :]) for k in range(CT)], DD,
                        ready=lambda k: mixed_ready(g, 0, k))
                mix(g, 2)
                mix(g, 3)
                wait_drained(pe, g, "decay_in")
                for c in range(CT):
                    product(g, f"proj0_{c}", [(dw2[:, c * P:(c + 1) * P], dl[:, :])])
                wait_drained(pe, g, "lora1")
                mix(g, 4)
                if first:
                    pe.wait_ge(w_in[1], 16 * 3)
                for f in (2, 1, 3):
                    product(g, f"proj{f}_0", proj_operands(f"proj{f}_0"), ready=lambda k: mixed_ready(g, f, k))
                if first:
                    pe.wait_ge(spread_ready, 1)
                    pe.wait_ge(w_in[2], 16 * (len(SELS) - 1))
                    pe.wait_ge(w_in[3], 16 * 5)
                for m in range(STEPS + LAG):
                    c, j = m // S, m % S
                    if m < STEPS:
                        scan_bcast(g, m)
                    if m >= LAG:
                        scan_sum(g, m - LAG)
                    if m >= STEPS:
                        continue
                    name, k = beside_scan(c)[j // 4], j % 4
                    if name:
                        lhsT, rhs = proj_operands(name)[k]
                        if k == 0:
                            claim(g, name)
                        if name == "proj4_0":
                            mixed_ready(g, 4, k)
                        ins = pe.matmul(gbank(name)[:, :], lhsT, rhs, start=(k == 0), stop=(k == CT - 1))
                        if k == CT - 1:
                            ins.then_inc(filled, 1)
                    if j == 3:
                        pe.wait_ge(bonus_in, at(g, CT, c + 1))
                        product(g, f"bonus_{c}", [(sel["headsum"][:, :], rkf)])
                    if j == 7 and c >= 1:
                        center(g, c - 1)
                    if j == 11 and c >= 1:
                        variance(g, c - 1)
                center(g, CT - 1)
                variance(g, CT - 1)
                pe.wait_ge(yg_ready, at(g, CT, CT))
                for b in range(GB):
                    product(g, f"wo_{b}", [(yg[:, k, b * P:(b + 1) * P], mat["Wo"][:, k, :]) for k in range(CT)])
                pe.wait_ge(normed[1], at(g, GB, GB))
                for c in range(CT):
                    turn(g, f"tr2_{c}", [xn[:, b, c * P:(c + 1) * P] for b in range(GB)])
                for c in range(CT):
                    product(g, f"key_{c}", [(mat["fWk"][:, k, c * P:(c + 1) * P], xk2[:, k, :]) for k in range(CT)],
                            ready=lambda k: pe.wait_ge(xk2_ready, at(g, CT, k + 1)) if c == 0 else None)
                front(g + 1)
                pe.wait_ge(xr2_ready, at(g, CT, CT))
                for b in range(GB):
                    product(g, f"recept_{b}", [(xr2[:, k, b * P:(b + 1) * P], mat["fWr"][:, k, :]) for k in range(CT)])
                    if b == 0:
                        wait_drained(pe, g, "key_3")
                    product(g, f"value_{b}", [(kk[:, k, b * P:(b + 1) * P], mat["fWv"][:, k, :]) for k in range(CT)])

            pe.wait_ge(ident_in, 16)
            front(0)
            pe.wait_ge(w_in[0], 16 * 4)
            group(0, True)
            with pe.Fori(1, NG) as g:
                group(g)

        @block.scalar
        def _(act):
            act.wait_ge(vec_in, 16)
            act.wait_ge(preset, 7)

            def layernorm_rstd(g, n, part):
                bs = slice(0, GB - 1) if part == 0 else slice(GB - 1, GB)
                act.wait_ge(stat[n], at(g, 2 * GB, 2 * GB - 2 + 2 * part))
                act.activation(lnv[:, n, bs], mv[:, n, bs, 1], ACT.Ln, bias=eps[:, :]).then_inc(lnv_done[n], 1)
                act.wait_ge(lnv_done[n], at(g, 2, part + 1))
                act.activation(rstd[:, n, bs], lnv[:, n, bs], ACT.Exp, scale=-0.5).then_inc(rstd_done[n], 1)

            def channel_major(g, n, w, b, c):
                wait_filled(act, g, f"tr{n}_{c}")
                act.activation(token_view[c], b3(gbank(f"tr{n}_{c}")[:, :]), ACT.Identity, bias=v_(b, c),
                               scale=v_(w, c)).then_inc(drained["act"], 1)

            def move(g, name, dst, func=ACT.Copy, rows=P):
                wait_filled(act, g, name)
                src = gbank(name)[0:rows, :]
                act.activation(dst, b3(src) if len(dst.shape) == 3 else src, func).then_inc(drained["act"], 1)

            def front_state(g):
                wait_filled(act, g, "state")
                act.activation(st_cols[:, :, :, :].rearrange("p c j b -> p c (j b)"),
                               gbank("state")[:, :].rearrange("p (c n) -> p c n", c=CT)[:, :, 0:2 * GB],
                               ACT.Copy).then_inc(drained["act"], 1)
                wait_drained(act, g, "state")
                wait_if(act, xk2_ready, at(g, CT, 0))
                wait_if(act, xr2_ready, at(g, CT, 0))
                act.activation(xa[:, :, :, 0], st_cols[:, :, 1, :], ACT.Copy).then_inc(edge[0], 1)
                for c in range(CT):
                    channel_major(g, 1, "ln1_w", "ln1_b", c)

            def take_v(g, c):
                if c >= 2:
                    wait_drained(act, g, f"bonus_{c - 2}")
                move(g, f"proj2_{c}", v_pad[:, c % 2, :, 1:P + 1])
                wait_drained(act, g, f"proj2_{c}")
                wait_if(act, bcast, at(g, STEPS, max((c - 1) * S, 0)))
                act.activation(b3(v_parts[:, c % 2, 0, :]), v_pad[:, c % 2, :, 0:P], ACT.Copy).then_inc(v_high, 1)

            def center_square(g, c):
                name = f"center_{c}"
                wait_filled(act, g, name)
                act.activation(ysq, gbank(name)[:, :], ACT.Square).then_inc(squared, 1)
                act.activation(y_sb[:, :], gbank(name)[:, :], ACT.Copy).then_inc(drained["act"], 1)

            def inverse_root(g, c):
                name = f"var_{c}"
                wait_filled(act, g, name)
                act.activation(gbank(name)[:, :], gbank(name)[:, :], ACT.Ln, bias=eps[:, :]).then_inc(rooted, 1)
                act.wait_ge(rooted, at(g, CT, c + 1))
                act.activation(rs[:, :], gbank(name)[:, :], ACT.Exp, scale=-0.5).then_inc(drained["act"], 1)

            def group(g):
                move(g, "lora0", th0[:, :], ACT.Tanh)
                move(g, "lora1", th1[0:DM, :], ACT.Tanh, DM)
                move(g, "decay_in", dl[0:DD, :], ACT.Tanh, DD)
                for c in range(CT):
                    name = f"proj0_{c}"
                    wait_filled(act, g, name)
                    act.activation(gbank(name)[:, :], gbank(name)[:, :], ACT.Exp,
                                   bias=v_("time_decay", c)).then_inc(doubled, 1)
                    act.wait_ge(doubled, at(g, CT, c + 1))
                    act.activation(w_sh[:, c, :, 1:P], b3(gbank(name)[:, :])[:, :, 0:P - 1], ACT.Exp,
                                   scale=-1.0).then_inc(drained["act"], 1)
                take_v(g, 0)
                move(g, "proj1_0", k_pad[:, 0, :, 1:P + 1])
                move(g, "proj3_0", r_sb[:, 0, :, :])
                act.wait_ge(s0_landed, at(g, 16 * GB, 16 * GB))
                for m in range(STEPS):
                    c, j = m // S, m % S
                    act.wait_ge(bcast, at(g, STEPS, m + 1))
                    act.activation(vb[m % RING][:, :, 0], s0[:, :, c, 4 * (j % 4) + j // 4],
                                   ACT.Copy).then_inc(s0_put, 1)
                    if j == 3 and c + 1 < CT:
                        take_v(g, c + 1)
                    if j == 7 and c >= 1:
                        move(g, f"proj4_{c - 1}", yg[:, c - 1, :], ACT.Silu)
                    if j == 8 and c >= 1:
                        center_square(g, c - 1)
                    if j == 11 and c + 1 < CT:
                        if c + 1 >= 2:
                            act.wait_ge(kv, at(g, STEPS, c * S))
                        move(g, f"proj1_{c + 1}", k_pad[:, (c + 1) % 2, :, 1:P + 1])
                    if j == 12 and c >= 1:
                        inverse_root(g, c - 1)
                    if j == 15:
                        if c + 1 < CT:
                            move(g, f"proj3_{c + 1}", r_sb[:, c + 1, :, :])
                        else:
                            move(g, "proj4_3", yg[:, 3, :], ACT.Silu)
                center_square(g, CT - 1)
                inverse_root(g, CT - 1)
                act.activation(xa[:, :, :, 0], st_cols[:, :, 0, :], ACT.Copy).then_inc(edge[1], 1)
                layernorm_rstd(g, 1, 0)
                layernorm_rstd(g, 1, 1)
                for c in range(CT):
                    channel_major(g, 2, "ln2_w", "ln2_b", c)
                for c in range(CT):
                    name = f"key_{c}"
                    wait_filled(act, g, name)
                    act.activation(gbank(name)[:, :], gbank(name)[:, :], ACT.Relu).then_inc(relu_done, 1)
                    act.wait_ge(relu_done, at(g, CT, c + 1))
                    act.activation(kk[:, c, :], gbank(name)[:, :], ACT.Square).then_inc(drained["act"], 1)
                    if c == 0:
                        layernorm_rstd(g + 1, 0, 0)
                        layernorm_rstd(g + 1, 0, 1)
                front_state(g + 1)
                for b in range(GB):
                    if b >= 2:
                        act.wait_ge(gated, at(g, GB, b - 1))
                    move(g, f"recept_{b}", rr[:, b % 2, :], ACT.Sigmoid)

            layernorm_rstd(0, 0, 0)
            layernorm_rstd(0, 0, 1)
            front_state(0)
            group(0)
            with act.Fori(1, NG) as g:
                group(g)

        @block.vector
        def _(dve):
            dve.memset(st_rows[:, :], 0.0).then_inc(preset, 1)
            dve.memset(eps[:, :], EPS).then_inc(preset, 1)
            dve.memset(k_pad[:, :, :, 0], 1.0).then_inc(preset, 1)
            dve.memset(v_pad[:, :, :, 0], 0.0).then_inc(preset, 1)
            dve.memset(th1[:, :], 0.0).then_inc(preset, 1)
            dve.memset(dl[:, :], 0.0).then_inc(preset, 1)
            dve.memset(spare[:, :], 0.0).then_inc(preset, 1)
            dve.wait_ge(preset, 7)
            dve.wait_ge(ident_in, 16)
            dve.tensor_copy(spread[:, :, :], sel["ident"][:, :, None].broadcast_to((P, P, S))).then_inc(spread_ready, 1)
            dve.wait_ge(vec_in, 16)

            def layernorm(g, n, rows, make=None):
                def aggregate(done, bs):
                    dve.wait_ge(stat[n], at(g, 2 * GB, done))
                    dve.memset(spare[:, :], 0.0)
                    for b in bs:
                        dve.bn_aggr(mv[:, n, b, :], stats[:, n, b, :]).then_inc(stat[n], 1)
                for b in range(GB):
                    if b == GB - 1:
                        aggregate(GB - 1, range(GB - 1))
                    if make:
                        make(b)
                    dve.bn_stats(stats[:, n, b, :], rows[:, b, :]).then_inc(stat[n], 1)
                aggregate(2 * GB - 1, [GB - 1])
                for b in range(GB):
                    if b == 0:
                        dve.wait_ge(rstd_done[n], at(g, 2, 1))
                    if b == GB - 1:
                        dve.wait_ge(rstd_done[n], at(g, 2, 2))
                    dve.tensor_scalar(xn[:, b, :], rows[:, b, :], mv[:, n, b, 0:1], rstd[:, n, b:b + 1],
                                      ALU.subtract, ALU.mult).then_inc(normed[n], 1)

            def front_norm(g):
                dve.wait_ge(x_landed, at(g, 16, 16))
                layernorm(g, 0, x_in)
                dve.wait_ge(normed[0], at(g, GB, GB))
                dve.memset(w_sh[:, :, :, 0], 0.0).then_inc(zeroed, 1)

            def front_shift(g):
                dve.wait_ge(edge[0], at(g, 1, 1))
                for c in range(CT):
                    wait_drained(dve, g, f"tr1_{c}")
                    dve.tensor_tensor(b3(sx[:, c, :]), shifted_view[c], token_view[c], ALU.subtract).then_inc(shifted, 1)
                for c in range(CT):
                    dve.wait_ge(shifted, at(g, CT, c + 1))
                    dve.scalar_tensor_tensor(out=b3(xxx[:, c, :]), in0=b3(sx[:, c, :]), scalar=v_("maa_x", c),
                                             in1=token_view[c], op0=ALU.mult, op1=ALU.add).then_inc(mixed_x, 1)

            def mix(g, f, name):
                def add_x(c):
                    wait_drained(dve, g, f"mix{f}_{c}")
                    dve.tensor_tensor(b3(mixed_in[f][:, c, :]), b3(mixt[:, c, :]), token_view[c],
                                      ALU.add).then_inc(mixed[1], 1)
                for c in range(CT):
                    wait_filled(dve, g, f"mix{f}_{c}")
                    if f == 0 and c == 0:
                        wait_if(dve, gated, at(g, GB, 0))
                    wait_if(dve, mixed[c % 2], reuse(g, NF * 2, f * 2 + c // 2, 2))
                    dve.scalar_tensor_tensor(out=mixt[:, c, :], in0=gbank(f"mix{f}_{c}")[:, :],
                                             scalar=v_(name, c), in1=sx[:, c, :], op0=ALU.add,
                                             op1=ALU.mult).then_inc(drained["dve"], 1)
                    if c == 2:
                        add_x(1)
                add_x(3)

            def v_rest(g, c):
                dve.wait_ge(v_high, at(g, CT, c + 1))
                dve.tensor_tensor(b3(v_parts[:, c % 2, 1, :]), v_pad[:, c % 2, :, 0:P],
                                  b3(v_parts[:, c % 2, 0, :]).bitcast(F32), ALU.subtract).then_inc(v_low, 1)

            def take_y(g, c):
                dve.wait_ge(summed, at(g, STEPS, (c + 1) * S))
                dve.tensor_tensor(y_sb[:, :], y_ps[:, :], bon[:, :], ALU.add).then_inc(y_done, 1)

            def scale_y(g, c):
                wait_drained(dve, g, f"var_{c}")
                wait_drained(dve, g, f"center_{c}")
                dve.scalar_tensor_tensor(out=z_sb, in0=y_sb[:, :], scalar=v_("gn_w", c),
                                         in1=rs[:, :], op0=ALU.mult, op1=ALU.mult).then_inc(z_done, 1)

            def gate_y(g, c):
                dve.wait_ge(z_done, at(g, CT, c + 1))
                wait_drained(dve, g, f"proj4_{c}")
                dve.scalar_tensor_tensor(out=yg[:, c, :], in0=z_sb, scalar=v_("gn_b", c),
                                         in1=yg[:, c, :], op0=ALU.add, op1=ALU.mult).then_inc(yg_ready, 1)

            def group(g):
                for f, name in enumerate(("maa_w", "maa_k", "maa_v", "maa_r", "maa_g")):
                    mix(g, f, name)
                v_rest(g, 0)
                for m in range(STEPS + 1):
                    c, j = m // S, m % S
                    if m < STEPS:
                        if j == 0:
                            wait_drained(dve, g, f"proj1_{c}")
                        dve.wait_ge(s0_put, at(g, STEPS, m + 1))
                        dve.tensor_tensor(vb[m % RING][:, :, :], vb[m % RING][:, :, :], k_pad[:, c % 2, :, 0:P],
                                          ALU.mult).then_inc(kv, 1)
                    if m >= 1:
                        n = m - 1
                        if n == 0:
                            dve.wait_ge(zeroed, at(g, 1, 1))
                            dve.wait_ge(mixed[0], at(g, NF * 2, NF * 2))
                        if n % S == 0:
                            wait_drained(dve, g, f"proj0_{n // S}")
                        dve.wait_ge(kv, at(g, STEPS, n + 1))
                        wait_if(dve, prodded, reuse(g, STEPS, n, RING))
                        dve.tensor_tensor_scan(states[:, n % RING, :, :].rearrange("p b l -> p (b l)"),
                                               w_sh[:, n // S, :, :].rearrange("p b l -> p (b l)"),
                                               vb[n % RING][:, :, :].rearrange("p b l -> p (b l)"),
                                               0.0, ALU.mult, ALU.add).then_inc(scanned, 1)
                    if m == STEPS:
                        continue
                    if j == 0:
                        wait_drained(dve, g, f"proj3_{c}")
                        if c >= 2:
                            dve.wait_ge(yg_ready, at(g, CT, c - 1))
                        dve.scalar_tensor_tensor(out=b3(rkf), in0=r_sb[:, c, :, :], scalar=v_("faaaa", c),
                                                 in1=k_pad[:, c % 2, :, 1:P + 1], op0=ALU.mult,
                                                 op1=ALU.mult).then_inc(bonus_in, 1)
                    if j == 3 and c >= 1:
                        take_y(g, c - 1)
                    if j == 6:
                        wait_filled(dve, g, f"bonus_{c}")
                        dve.tensor_tensor(b3(bon[:, :]), b3(gbank(f"bonus_{c}")[:, :]), v_pad[:, c % 2, :, 1:P + 1],
                                          ALU.mult).then_inc(drained["dve"], 1)
                    if j == 7 and c + 1 < CT:
                        v_rest(g, c + 1)
                    if j == 14 and c >= 1:
                        scale_y(g, c - 1)
                    if j == 15 and c >= 1:
                        gate_y(g, c - 1)
                take_y(g, CT - 1)
                scale_y(g, CT - 1)
                gate_y(g, CT - 1)

                def residual(b):
                    wait_filled(dve, g, f"wo_{b}")
                    dve.tensor_tensor(x1[:, b, :], gbank(f"wo_{b}")[:, :], x1[:, b, :],
                                      ALU.add).then_inc(drained["dve"], 1)
                    wait_drained(dve, g, f"wo_{b}")
                dve.wait_ge(res_landed, at(g, 16, 16))
                layernorm(g, 1, x1, residual)
                dve.wait_ge(edge[1], at(g, 1, 1))
                for c in range(CT):
                    wait_drained(dve, g, f"tr2_{c}")
                    dve.tensor_tensor(b3(sx[:, c, :]), shifted_view[c], token_view[c],
                                      ALU.subtract).then_inc(shifted2, 1)
                    dve.wait_ge(shifted2, at(g, CT, c + 1))
                    dve.scalar_tensor_tensor(out=b3(xk2[:, c, :]), in0=b3(sx[:, c, :]), scalar=v_("fmaa_k", c),
                                             in1=token_view[c], op0=ALU.mult, op1=ALU.add).then_inc(xk2_ready, 1)
                for c in range(CT):
                    dve.scalar_tensor_tensor(out=b3(xr2[:, c, :]), in0=b3(sx[:, c, :]), scalar=v_("fmaa_r", c),
                                             in1=token_view[c], op0=ALU.mult, op1=ALU.add).then_inc(xr2_ready, 1)
                front_norm(g + 1)
                front_shift(g + 1)
                for b in range(GB):
                    wait_filled(dve, g, f"value_{b}")
                    wait_drained(dve, g, f"recept_{b}")
                    dve.tensor_tensor(rr[:, b % 2, :], gbank(f"value_{b}")[:, :], rr[:, b % 2, :],
                                      ALU.mult).then_inc(drained["dve"], 1)
                    wait_drained(dve, g, f"value_{b}")
                    dve.tensor_tensor(x1[:, b, :], rr[:, b % 2, :], x1[:, b, :], ALU.add).then_inc(gated, 1)

            front_norm(0)
            front_shift(0)
            group(0)
            with dve.Fori(1, NG) as g:
                group(g)

        @block.gpsimd
        def _(pool):
            def group(g):
                for f in range(NF):
                    for c in (0, 2):
                        wait_drained(pool, g, f"mix{f}_{c}")
                        if c == 0 and f == 1:
                            wait_drained(pool, g, "lora1")
                        if c == 0 and f == 4:
                            wait_filled(pool, g, "decay_in")
                        pool.tensor_tensor(b3(mixed_in[f][:, c, :]), b3(mixt[:, c, :]), token_view[c],
                                           ALU.add).then_inc(mixed[0], 1)
                for m in range(STEPS):
                    if m % S == 0:
                        wait_drained(pool, g, f"proj3_{m // S}")
                    pool.wait_ge(scanned, at(g, STEPS, m + 1))
                    wait_if(pool, summed, reuse(g, STEPS, m, PRING))
                    pool.tensor_tensor(b3(prods[:, m % PRING, :]), states[:, m % RING, :, :],
                                       r_sb[:, m // S, :, :], ALU.mult).then_inc(prodded, 1)
            group(0)
            with pool.Fori(1, NG) as g:
                group(g)


def kernel(**inputs):
    import numpy as np
    import concourse.bacc as bacc
    from concourse.bass_utils import run_bass_kernel_spmd

    def arr(name):
        return np.asarray(inputs["L0_xattn_" + name])

    def perm(a, axis):
        a = np.moveaxis(a, axis, 0)
        a = a.reshape(CT, HT, S, *a.shape[1:]).swapaxes(1, 2).reshape(a.shape)
        return np.moveaxis(a, 0, axis)

    def tiles(a):
        return np.ascontiguousarray(a.reshape(CT, P, -1).transpose(1, 0, 2))

    arrays = {"x": np.ascontiguousarray(inputs["x"]), "ctx_in": np.ascontiguousarray(inputs["ctx_2048"])}
    cols = [perm(arr(n), 0) if n in ("gn_w", "gn_b") else arr(n).reshape(C) for n in VECS]
    arrays["vecs"] = np.ascontiguousarray(np.stack(cols).reshape(len(VECS), CT, P).transpose(2, 0, 1))
    for n in MATS:
        w = arr(n).T
        if n in ("Wv", "Wg"):
            w = perm(w, 1)
        if n == "Wo":
            w = perm(w, 0)
        arrays["m_" + n] = tiles(w)
    arrays["maa_w1"] = tiles(arr("maa_w1"))
    w2 = np.zeros((P, NF, C), np.float32)
    for f in range(NF):
        row = DM * (f % 4)
        w2[row:row + DM, f] = arr("maa_w2")[f]
    arrays["maa_w2"] = w2
    arrays["decay_w1"] = tiles(arr("decay_w1"))
    arrays["decay_w2"] = np.zeros((P, C), np.float32)
    arrays["decay_w2"][0:DD] = arr("decay_w2")

    head_n, s_n = np.arange(P) // S, np.arange(P) % S
    head_y = np.arange(P) % HT
    same_ny = (head_n[:, None] == head_y[None, :])
    same_yy = (head_y[:, None] == head_y[None, :])
    local = np.arange(32)
    gather = np.stack([(local // HT == i)[None, :] & (head_n[:, None] == (local % HT)[None, :]) for i in range(4)], 1)
    consts = {"ident": np.eye(P), "gather": gather.reshape(P, 128),
              "headsum": same_ny, "center": np.eye(P) - same_yy / S, "headmean": same_yy / S}
    for n in SELS:
        arrays["s_" + n] = np.ascontiguousarray(consts[n].astype(np.float32))

    nc = bacc.Bacc("TRN2", target_bir_lowering=False, num_devices=1)
    ap = {n: nc.dram_tensor("in_" + n, a.shape, F32, kind="ExternalInput").ap() for n, a in arrays.items()}
    shape = inputs["x"].shape
    out = nc.dram_tensor("out_y", shape, F32, kind="ExternalOutput").ap()
    rwkv_kernel(nc, ap["x"], ap["ctx_in"], ap["vecs"], {n: ap["m_" + n] for n in MATS}, ap["maa_w1"], ap["maa_w2"],
                ap["decay_w1"], ap["decay_w2"], {n: ap["s_" + n] for n in SELS}, out)
    r = run_bass_kernel_spmd(nc, [{"in_" + n: a for n, a in arrays.items()}], core_ids=[0])
    return r.results[0]["out_y"]
```

```python
from contextlib import ExitStack

import concourse.bass as bass
from concourse import mybir

F32 = mybir.dt.float32
F32R = mybir.dt.float32r
ALU = mybir.AluOpType
ACT = mybir.ActivationFunctionType

P = 128
GB = 4
T = GB * P
CT = 4
C = CT * P
S = 16
HT = P // S
DM, DD = 32, 64
EPS = 1e-5
NF = 5
BANKS = 3
STEPS = CT * S
RING = 4
PRING = 4
LAG = 5

VECS = ["ln1_w", "ln1_b", "ln2_w", "ln2_b", "maa_x", "maa_w", "maa_k", "maa_v", "maa_r", "maa_g",
        "time_decay", "faaaa", "gn_w", "gn_b", "fmaa_k", "fmaa_r"]
MATS = ["Wr", "Wk", "Wv", "Wg", "Wo", "fWk", "fWr", "fWv"]
ORDER = [0, 2, 1, 4, 3]
ROUTE_T, ROUTE_V, PICK = 4 * 5 * DM, 2 * 3 * 64, 64
SELS = ["ident", "gather", "headsum", "center", "headmean"]


PROJ_STEPS = [0, 1, 2, 3, 6, 7, 8, 9, 11, 12, 13, 14]


def projection_beside(c, j):
    if c == CT:
        return "proj4_3", j
    if j not in PROJ_STEPS:
        return None, 0
    n, k = divmod(PROJ_STEPS.index(j), CT)
    return ([f"proj2_{c + 1}", f"proj1_{c + 1}", f"proj3_{c + 1}"] if c + 1 < CT else
            ["proj4_0", "proj4_1", "proj4_2"])[n], k


def products_beside(c, j):
    if j == 4:
        return [f"bonus_{c}"]
    if j == 5 and c:
        return [f"center_{c - 1}"]
    if j == 10:
        return ([f"var_{c - 1}"] if c else []) + ([f"route_v{c + 1}_0"] if c + 1 < CT else [])
    if j == 15:
        return [f"route_v{c + 1}_1"] if c + 1 < CT else []
    return []


def general_uses():
    ours, ahead = [], []

    def now(*us):
        ours.extend(us)

    def nxt(*us):
        ours.extend(us)
        ahead.extend(us)

    for c in range(CT):
        for j in range(S):
            name, k = projection_beside(c, j)
            now(*([name] if name and k == 0 else []), *products_beside(c, j))
    now("proj4_3", "center_3", "var_3")
    nxt("state", *[f"tr1_{c}" for c in range(CT)], "lora0", "lora1")
    now("key_0")
    nxt("route_t0")
    now("key_1")
    nxt("route_t2")
    now("key_2", "key_3")
    nxt("route_t1")
    now("recept_0")
    nxt("route_t3")
    now("value_0")
    nxt("decay_in")
    now("recept_1")
    nxt("route_t4")
    now("value_1")
    nxt("proj2_0")
    now("recept_2", "value_2")
    nxt("route_v0_0")
    now("recept_3")
    nxt("route_v0_1", "proj0_0")
    now("value_3")
    nxt("proj0_1", "proj0_2", "proj1_0", "proj0_3", "proj3_0")
    by_dve = ("bonus", "value", "proj4")
    return ours, ahead, {u: "dve" if u.startswith(by_dve) else "act" for u in ours}


def rwkv_kernel(nc, x, ctx_in, vecs, mats, maa_w1, maa_w2, decay_w1, decay_w2, sels, routes, out):
    NB = x.shape[0]
    NG = NB // GB
    names, ahead_names, who = general_uses()
    order = {u: n for n, u in enumerate(names)}
    users = {w: [u for u in names if who[u] == w] for w in ("act", "dve")}

    with ExitStack() as ctx:
        def sb(name, shape, dt=F32):
            return ctx.enter_context(nc.sbuf_tensor(name, shape, dt))

        def sem(name):
            return ctx.enter_context(nc.semaphore(name))

        vec = sb("vec", [P, len(VECS), CT])
        mat = {n: sb("m_" + n, [P, CT, C]) for n in MATS}
        w1 = sb("w1", [P, CT, NF * DM])
        w2 = sb("w2", [P, NF, C], F32R)
        dw1 = sb("dw1", [P, CT, DD])
        dw2 = sb("dw2", [P, C])
        sel = {n: sb("s_" + n, [P, P]) for n in SELS}
        spread = sb("spread", [P, 64, S], F32R)
        route_t = sb("route_t", [P, 4, 5 * DM], F32R)
        route_v = sb("route_v", [P, 2, 3 * 64], F32R)
        eps = sb("eps", [P, 1])
        spare = sb("spare", [P, 1])
        warm = sb("warm", [P, 3])
        x1 = sb("x1", [P, GB, C])
        st_cols = sb("st_cols", [P, CT, 2, GB])
        s0 = sb("s0", [P, GB, CT, S])
        stats = sb("stats", [P, 2, GB, 6])
        mv = sb("mv", [P, 2, GB, 2])
        lnv = sb("lnv", [P, 2, GB])
        rstd = sb("rstd", [P, 2, GB])
        xa = sb("xa", [P, CT, GB, P + 1])
        sx = sb("sx", [P, CT, T])
        buf = [sb(f"buf{i}", [P, CT, T]) for i in range(4)]
        xn = [buf[1], buf[0]]
        xxx = buf[1]
        mixed_in = [buf[0], buf[1], buf[2], buf[3], buf[0]]
        xk2, xr2 = buf[2], buf[3]
        bon = [xa[:, i, :, 0:P] for i in range(2)]
        rs = sb("rs", [P, T])
        th1 = rs
        dl = rs
        y_sb = sb("y_sb", [P, T])
        th0 = y_sb
        stage = [b[:, :, :].rearrange("p c t -> p (c t)") for b in buf[2:4]]
        w_sh = sb("w_sh", [P, CT, GB, P])
        x_in = w_sh[:, :, :, :].rearrange("p c b l -> p c (b l)")
        k_pad = sb("k_pad", [P, 2, GB, P + 1])
        v_pad = sb("v_pad", [P, 2, GB, P + 1])
        parts = sb("parts", [P, 2, T], F32R)
        routed = sb("routed", [P, 4, T], F32R)
        st_rows = v_pad[:, 0, :, 1:P + 1]
        r_sb = sb("r_sb", [P, CT, GB, P])
        kk = r_sb[:, :, :, :].rearrange("p c b l -> p c (b l)")
        yg = sb("yg", [P, CT, GB, P + 1])
        states = sb("states", [P, RING, GB, P])
        mixt = states[:, :, :, :].rearrange("p r b l -> p r (b l)")
        sx2 = mixt
        rr = k_pad[:, :, :, 1:P + 1]
        prods = sx[:, 0:PRING, :]
        rkf = xa[:, 2, :, 0:P]
        ysq = xa[:, 3, :, 0:P]
        bank = [ctx.enter_context(nc.psum_tensor(f"gen{i}", [P, T], F32)) for i in range(BANKS)]
        vb = [ctx.enter_context(nc.psum_tensor(f"vb{i}", [P, GB, P], F32)) for i in range(RING)]
        y_ps = ctx.enter_context(nc.psum_tensor("y_ps", [P, T], F32))

        vec_in = sem("vec_in")
        ident_in = sem("ident_in")
        w_in = [sem(f"w_in{i}") for i in range(4)]
        x_landed = [sem(f"x_landed{b}") for b in range(GB)]
        st_landed, s0_landed, res_landed, stored = (
            sem(n) for n in ("st_landed", "s0_landed", "res_landed", "stored"))
        preset = sem("preset")
        zeroed = sem("zeroed")
        stage_in = sem("stage_in")
        converted = sem("converted")
        filled = sem("filled")
        drained = {"act": sem("act_drained"),
                   "dve": sem("dve_drained")}
        stat, lnv_done, rstd_done, normed, edge = (
            [sem(f"{n}{i}") for i in (1, 2)] for n in ("stat", "lnv_done", "rstd_done", "normed", "edge"))
        shifted = sem("shifted")
        mix_filled = sem("mix_filled")
        mix_drained = sem("mix_drained")
        mixed_x = sem("mixed_x")
        mixed = [sem("mixed_pool"), sem("mixed_dve")]
        doubled = sem("doubled")
        part_high, part_low = sem("part_high"), sem("part_low")
        bcast, s0_put, kv, scanned, prodded, summed = (
            sem(n) for n in ("bcast", "s0_put", "kv", "scanned", "prodded", "summed"))
        bonus_in = sem("bonus_in")
        y_done = sem("y_done")
        squared = sem("squared")
        rs_done = sem("rs_done")
        z_done = sem("z_done")
        gate_done = sem("gate_done")
        wo_filled = sem("wo_filled")
        residual_done = sem("residual_done")
        turned2, xc_done = sem("turned2"), sem("xc_done")
        shifted2 = sem("shifted2")
        xk2_ready, xr2_ready = sem("xk2_ready"), sem("xr2_ready")
        relu_done = sem("relu_done")
        gated = sem("gated")
        block = ctx.enter_context(nc.Block())

        def v_(name, c):
            return vec[:, VECS.index(name), c:c + 1]

        def at(g, count, n):
            return g * count + n

        def reuse(g, count, n, depth):
            return g * count + max(n + 1 - depth, 0)

        def wait_if(eng, s, value):
            if not (isinstance(value, int) and value <= 0):
                eng.wait_ge(s, value)

        def general_count(g, name, counted):
            ahead = [u for u in counted if u in ahead_names]
            if name in ahead_names:
                if isinstance(g, int) and g == 0:
                    return ahead.index(name) + 1
                g = g - 1
            return g * len(counted) + len(ahead) + counted.index(name) + 1

        def wait_filled(eng, g, name):
            eng.wait_ge(filled, general_count(g, name, names))

        def wait_drained(eng, g, name):
            eng.wait_ge(drained[who[name]], general_count(g, name, users[who[name]]))

        def mix_count(g, f, c):
            return at(g, NF * CT, ORDER.index(f) * CT + c + 1)

        def gbank(name):
            return bank[order[name] % BANKS]

        shifted_view = [xa[:, c, :, 0:P] for c in range(CT)]
        token_view = [xa[:, c, :, 1:P + 1] for c in range(CT)]
        shifted_view2 = [yg[:, c, :, 0:P] for c in range(CT)]
        token_view2 = [yg[:, c, :, 1:P + 1] for c in range(CT)]

        def b3(ap):
            return ap.rearrange("p (b l) -> p b l", b=GB)

        @block.sync
        def _(sp):
            def load_x(g, b):
                sp.dma_start(x_in[:, b, :], x[bass.ds(g * GB + b, 1)].rearrange("b l c -> (b l) c")).then_inc(
                    x_landed[b], 16)

            def load_state(g):
                for j in range(2):
                    sp.dma_start(st_rows[j * GB:(j + 1) * GB], ctx_in[bass.ds(g * GB, GB), j, :].rearrange(
                        "b (c n) -> b c n", c=CT)).then_inc(st_landed, 16)

            def load_s0(g):
                wait_if(sp, s0_put, at(g, STEPS, 0))
                for b in range(GB):
                    sp.dma_start(s0[:, b, :, :], ctx_in[bass.ds(g * GB + b, 1), 2:2 + S, :].rearrange(
                        "b (ct hp) (hl s t) -> (b hp hl s) ct t", ct=CT, hl=2, t=S)).then_inc(s0_landed, 16)

            def load_residual(g):
                wait_if(sp, stored, at(g, 16 * GB, 0))
                sp.dma_start(x1[:, :, :], x[bass.ds(g * GB, GB)].rearrange("b l c -> l b c")).then_inc(res_landed, 16)

            def store(g):
                for b in range(GB):
                    sp.wait_ge(gated, at(g, GB, b + 1))
                    sp.dma_start(out[bass.ds(g * GB + b, 1)].rearrange("b l c -> (b l) c"),
                                 x1[:, b, :]).then_inc(stored, 16)

            for b in range(GB):
                load_x(0, b)
            sp.wait_ge(preset, 1)
            load_state(0)
            sp.dma_start(sel["ident"][:, :], sels["ident"]).then_inc(ident_in, 16)
            sp.dma_start(vec[:, :, :], vecs).then_inc(vec_in, 16)
            sp.dma_start(stage[0], maa_w2[:, 0:4 * C]).then_inc(stage_in, 16)
            sp.dma_start(stage[1][:, 0:C], maa_w2[:, 4 * C:5 * C]).then_inc(stage_in, 16)
            sp.dma_start(stage[1][:, C:C + ROUTE_T + ROUTE_V + PICK], routes).then_inc(stage_in, 16)
            for i, group in enumerate([
                    [(w1[:, :, :], maa_w1), (dw1[:, :, :], decay_w1), (dw2[:, :], decay_w2)],
                    [(mat[n][:, :, :], mats[n]) for n in ("Wv", "Wk", "Wr")],
                    [(sel[n][:, :], sels[n]) for n in SELS[1:]],
                    [(mat[n][:, :, :], mats[n]) for n in ("Wg", "Wo", "fWk", "fWr", "fWv")]]):
                for dst, src in group:
                    sp.dma_start(dst, src).then_inc(w_in[i], 16)
                if i == 1:
                    load_s0(0)
                    load_residual(0)

            def after(g, last):
                nxt = g if last else g + 1
                for b in range(GB):
                    sp.wait_ge(scanned, at(g, STEPS, (b + 1) * S))
                    if b == 2:
                        load_state(nxt)
                    load_x(nxt, b)
                if not last:
                    load_s0(g + 1)
                store(g)
                if not last:
                    load_residual(g + 1)
            after(0, False)
            with sp.Fori(1, NG - 1) as g:
                after(g, False)
            after(NG - 1, True)
            sp.wait_ge(stored, 16 * GB * NG)

        @block.tensor
        def _(pe):
            def claim(g, name):
                same = [u for u in names if order[u] % BANKS == order[name] % BANKS]
                same_ahead = [u for u in same if u in ahead_names]
                n = same.index(name)
                if name in ahead_names and isinstance(g, int) and g == 0:
                    n = same_ahead.index(name)
                    if n:
                        wait_drained(pe, 0, same_ahead[n - 1])
                    return
                it = g - 1 if name in ahead_names else g
                if n == 0 and isinstance(it, int) and it == 0:
                    wait_drained(pe, 0, same_ahead[-1])
                    return
                it = it if n else it - 1
                wait_drained(pe, it + 1 if same[n - 1] in ahead_names else it, same[n - 1])

            def product(g, name, pairs, rows=P, ready=None):
                claim(g, name)
                for k, (lhsT, rhs) in enumerate(pairs):
                    if ready:
                        ready(k)
                    out_ps = gbank(name)[0:rows, :]
                    ins = pe.matmul(b3(out_ps) if len(rhs.shape) == 3 else out_ps, lhsT, rhs, start=(k == 0),
                                    stop=(k == len(pairs) - 1))
                ins.then_inc(filled, 1)

            def turn(g, name, srcs):
                claim(g, name)
                for n, src in enumerate(srcs):
                    ins = pe.transpose(gbank(name)[:, n * P:(n + 1) * P], src, sel["ident"][:, :])
                ins.then_inc(filled, 1)

            def route_ranks(g, f):
                pe.wait_ge(part_low, at(g, 2 + CT, 1 if f < 4 else 2))
                product(g, f"route_t{f}", [(route_t[:, f % 4, 0:P], parts[:, 0, :]),
                                           (route_t[:, f % 4, DM:DM + P], parts[:, 1, :])])

            def route_half(g, c, h):
                pe.wait_ge(part_low, at(g, 2 + CT, 3 + c))
                product(g, f"route_v{c}_{h}", [(route_v[:, h, 64:64 + P], parts[:, 0, :]),
                                               (route_v[:, h, 0:P], parts[:, 1, :])])

            def mix(g, f, half):
                wait_drained(pe, g, f"route_t{f}")
                for c in (2 * half, 2 * half + 1):
                    if f != ORDER[0]:
                        pe.wait_ge(mix_drained, mix_count(g, ORDER[ORDER.index(f) - 1], c))
                    pe.matmul(vb[c][:, :, :], w2[:, f, c * P:(c + 1) * P], b3(routed[:, f % 4, :]), start=True,
                              stop=True).then_inc(mix_filled, 1)

            def mixed_ready(g, f, k):
                pe.wait_ge(mixed[k % 2], at(g, NF * CT // 2, ORDER.index(f) * CT // 2 + k // 2 + 1))

            def proj_operands(name):
                f, c = int(name[4]), int(name[6])
                m = mat[{1: "Wk", 2: "Wv", 3: "Wr", 4: "Wg"}[f]]
                return [(m[:, k, c * P:(c + 1) * P], mixed_in[f][:, k, :]) for k in range(CT)]

            def turn_state(g):
                pe.wait_ge(st_landed, at(g, 32, 32))
                turn(g, "state", [st_rows[:, c, :] for c in range(CT)])

            def front(g):
                pe.wait_ge(normed[0], at(g, GB, GB))
                for c in range(CT):
                    turn(g, f"tr1_{c}", [xn[0][:, b, c * P:(c + 1) * P] for b in range(GB)])

            def scan_bcast(g, m):
                c, j = m // S, m % S
                t = 4 * (j % 4) + j // 4
                if j == 0:
                    wait_drained(pe, g, f"route_v{c}_1")
                wait_if(pe, scanned, reuse(g, STEPS, m, RING))
                ins = pe.matmul(vb[m % RING][:, :, :],
                                spread[:, t % 8 * HT:(t % 8 + 1) * HT, :].rearrange("p h s -> p (h s)"),
                                b3(routed[:, 2 * (c % 2) + t // 8, :]), start=True, stop=True)
                ins.then_inc(bcast, 1)

            def scan_sum(g, m):
                c, i, q = m // S, m % S // 4, m % 4
                if m % S == 0:
                    wait_if(pe, y_done, at(g, CT, c))
                pe.wait_ge(prodded, at(g, STEPS, m + 1))
                pe.matmul(y_ps[32 * q:32 * q + 32, :], sel["gather"][:, 32 * i:32 * i + 32],
                          prods[:, m % PRING, :], start=(i == 0), stop=(i == 3)).then_inc(summed, 1)

            def center(g, c):
                pe.wait_ge(y_done, at(g, CT, c + 1))
                product(g, f"center_{c}", [(sel["center"][:, :], y_sb[:, :])])

            def variance(g, c):
                pe.wait_ge(squared, at(g, CT, c + 1))
                product(g, f"var_{c}", [(sel["headmean"][:, :], ysq)])

            def beside(g, name, c):
                if name.startswith("bonus"):
                    pe.wait_ge(bonus_in, at(g, CT, c + 1))
                    product(g, name, [(sel["headsum"][:, :], rkf)])
                elif name.startswith("center"):
                    center(g, c - 1)
                elif name.startswith("var"):
                    variance(g, c - 1)
                else:
                    route_half(g, c + 1, int(name[-1]))

            def wo(g, b, k):
                wait_drained(pe, g, f"proj4_{k}")
                ins = pe.matmul(vb[b][:, :, :].rearrange("p b l -> p (b l)"), yg[:, k, b, 1:P + 1],
                                mat["Wo"][:, k, :], start=(k == 0), stop=(k == CT - 1))
                if k == CT - 1:
                    ins.then_inc(wo_filled, 1)

            def turn_second(g):
                for b in range(GB):
                    pe.wait_ge(normed[1], at(g, GB, b + 1))
                    for c in range(CT):
                        ins = pe.transpose(vb[c][:, b, :], xn[1][:, b, c * P:(c + 1) * P], sel["ident"][:, :])
                        if b == GB - 1:
                            ins.then_inc(turned2, 1)

            def key(g, c):
                product(g, f"key_{c}", [(mat["fWk"][:, k, c * P:(c + 1) * P], xk2[:, k, :]) for k in range(CT)],
                        ready=lambda k: pe.wait_ge(xk2_ready, at(g, CT, k + 1)) if c == 0 else None)

            def recept(g, b):
                if b == 0:
                    pe.wait_ge(xr2_ready, at(g, CT, CT))
                product(g, f"recept_{b}", [(xr2[:, k, b * P:(b + 1) * P], mat["fWr"][:, k, :]) for k in range(CT)])

            def value(g, b):
                if b == 0:
                    wait_drained(pe, g, "key_3")
                product(g, f"value_{b}", [(kk[:, k, b * P:(b + 1) * P], mat["fWv"][:, k, :]) for k in range(CT)])

            def decay(g, c):
                product(g, f"proj0_{c}", [(dw2[:, c * P:(c + 1) * P], dl[:, :])])

            def ahead(g, before=None):
                def prev(work, n):
                    if before is not None:
                        work(before, n)
                product(g, "lora0", [(w1[:, k, 0:P], xxx[:, k, :]) for k in range(CT)],
                        ready=lambda k: pe.wait_ge(mixed_x, at(g, CT, k + 1)))
                product(g, "lora1", [(w1[:, k, P:P + DM], xxx[:, k, :]) for k in range(CT)], DM)
                prev(key, 0)
                route_ranks(g, 0)
                prev(key, 1)
                route_ranks(g, 2)
                mix(g, 0, 0)
                prev(key, 2)
                mix(g, 0, 1)
                prev(key, 3)
                route_ranks(g, 1)
                prev(recept, 0)
                route_ranks(g, 3)
                mix(g, 2, 0)
                prev(value, 0)
                mix(g, 2, 1)
                product(g, "decay_in", [(dw1[:, k, :], mixed_in[0][:, k, :]) for k in range(CT)], DD,
                        ready=lambda k: mixed_ready(g, 0, k))
                prev(recept, 1)
                route_ranks(g, 4)
                mix(g, 1, 0)
                prev(value, 1)
                mix(g, 1, 1)
                if before is None:
                    pe.wait_ge(w_in[1], 16 * 3)
                product(g, "proj2_0", proj_operands("proj2_0"), ready=lambda k: mixed_ready(g, 2, k))
                prev(recept, 2)
                mix(g, 4, 0)
                prev(value, 2)
                mix(g, 4, 1)
                route_half(g, 0, 0)
                prev(recept, 3)
                route_half(g, 0, 1)
                wait_drained(pe, g, "decay_in")
                decay(g, 0)
                mix(g, 3, 0)
                prev(value, 3)
                decay(g, 1)
                mix(g, 3, 1)
                decay(g, 2)
                product(g, "proj1_0", proj_operands("proj1_0"), ready=lambda k: mixed_ready(g, 1, k))
                decay(g, 3)
                product(g, "proj3_0", proj_operands("proj3_0"), ready=lambda k: mixed_ready(g, 3, k))

            def group(g, first=False):
                if first:
                    pe.wait_ge(w_in[2], 16 * (len(SELS) - 1))
                    pe.wait_ge(w_in[3], 16 * 5)
                for m in range(STEPS + LAG):
                    c, j = m // S, m % S
                    if m < STEPS:
                        scan_bcast(g, m)
                    name, k = projection_beside(c, j)
                    if name and k < CT:
                        lhsT, rhs = proj_operands(name)[k]
                        if k == 0:
                            claim(g, name)
                        if name == "proj4_0":
                            mixed_ready(g, 4, k)
                        ins = pe.matmul(gbank(name)[:, :], lhsT, rhs, start=(k == 0), stop=(k == CT - 1))
                        if k == CT - 1:
                            ins.then_inc(filled, 1)
                    if m >= LAG:
                        scan_sum(g, m - LAG)
                    if m >= STEPS:
                        continue
                    for name in products_beside(c, j):
                        beside(g, name, c)
                wo(g, 0, 0)
                wo(g, 0, 1)
                center(g, CT - 1)
                wo(g, 1, 0)
                wo(g, 1, 1)
                wo(g, 2, 0)
                variance(g, CT - 1)
                wo(g, 2, 1)
                wo(g, 3, 0)
                wo(g, 3, 1)
                for b in range(GB):
                    wo(g, b, 2)
                turn_state(g + 1)
                for b in range(GB):
                    wo(g, b, 3)
                front(g + 1)
                turn_second(g)
                ahead(g + 1, g)

            pe.wait_ge(ident_in, 16)
            turn_state(0)
            front(0)
            pe.wait_ge(w_in[0], 16 * 3)
            pe.wait_ge(converted, 7)
            ahead(0)
            group(0, True)
            with pe.Fori(1, NG) as g:
                group(g)

        @block.scalar
        def _(act):
            act.wait_ge(vec_in, 16)
            act.wait_ge(preset, 5)

            def take_ln(g, n):
                act.wait_ge(stat[n], at(g, 2 * GB, 2 * GB))
                act.activation(lnv[:, n, :], mv[:, n, :, 1], ACT.Ln, bias=eps[:, :]).then_inc(lnv_done[n], 1)

            def take_rstd(g, n):
                act.wait_ge(lnv_done[n], at(g, 1, 1))
                act.activation(rstd[:, n, :], lnv[:, n, :], ACT.Exp, scale=-0.5).then_inc(rstd_done[n], 1)

            def load_table(func):
                n = [ACT.Ln, ACT.Exp, ACT.Silu].index(func)
                act.activation(warm[:, n:n + 1], eps[:, :], func)

            def move(g, name, dst, func=ACT.Copy, rows=P):
                wait_filled(act, g, name)
                src = gbank(name)[0:rows, :]
                act.activation(dst, b3(src) if len(dst.shape) == 3 else src, func).then_inc(drained["act"], 1)

            def take_state(g):
                wait_filled(act, g, "state")
                act.activation(st_cols[:, :, :, :].rearrange("p c j b -> p c (j b)"),
                               gbank("state")[:, :].rearrange("p (c n) -> p c n", c=CT)[:, :, 0:2 * GB],
                               ACT.Copy).then_inc(drained["act"], 1)
                wait_drained(act, g, "state")
                act.activation(xa[:, :, :, 0], st_cols[:, :, 1, :], ACT.Copy).then_inc(edge[0], 1)

            def first_norm(g):
                for c in range(CT):
                    wait_filled(act, g, f"tr1_{c}")
                    act.activation(token_view[c], b3(gbank(f"tr1_{c}")[:, :]), ACT.Identity, bias=v_("ln1_b", c),
                                   scale=v_("ln1_w", c)).then_inc(drained["act"], 1)

            def second_norm(g):
                for c in range(CT):
                    act.wait_ge(turned2, at(g, CT, c + 1))
                    act.activation(token_view2[c], vb[c][:, :, :], ACT.Identity, bias=v_("ln2_b", c),
                                   scale=v_("ln2_w", c)).then_inc(xc_done, 1)

            def take_v(g, c):
                if c >= 2:
                    wait_drained(act, g, f"bonus_{c - 2}")
                move(g, f"proj2_{c}", v_pad[:, c % 2, :, 1:P + 1])
                wait_drained(act, g, f"proj2_{c}")
                wait_filled(act, g, f"route_v{c - 1}_1" if c else "route_t4")
                act.activation(b3(parts[:, 0, :]), v_pad[:, c % 2, :, 0:P], ACT.Copy).then_inc(part_high, 1)

            def silu(g, c):
                name = f"proj4_{c}"
                wait_filled(act, g, name)
                act.activation(gbank(name)[:, :], gbank(name)[:, :], ACT.Silu).then_inc(gate_done, 1)

            def center_square(g, c):
                name = f"center_{c}"
                wait_filled(act, g, name)
                act.activation(ysq, b3(gbank(name)[:, :]), ACT.Square).then_inc(squared, 1)
                act.activation(y_sb[:, :], gbank(name)[:, :], ACT.Copy).then_inc(drained["act"], 1)

            def take_ln_var(g, c):
                if c:
                    act.wait_ge(z_done, at(g, CT, c))
                name = f"var_{c}"
                wait_filled(act, g, name)
                act.activation(rs[:, :], gbank(name)[:, :], ACT.Ln, bias=eps[:, :]).then_inc(drained["act"], 1)

            def inverse_root(g, c):
                wait_drained(act, g, f"var_{c}")
                act.activation(rs[:, :], rs[:, :], ACT.Exp, scale=-0.5).then_inc(rs_done, 1)

            def key(g, c):
                name = f"key_{c}"
                wait_filled(act, g, name)
                act.activation(gbank(name)[:, :], gbank(name)[:, :], ACT.Relu).then_inc(relu_done, 1)
                act.wait_ge(relu_done, at(g, CT, c + 1))
                act.activation(kk[:, c, :], gbank(name)[:, :], ACT.Square).then_inc(drained["act"], 1)

            def recept(g, b):
                if b >= 2:
                    act.wait_ge(gated, at(g, GB, b - 1))
                move(g, f"recept_{b}", rr[:, b % 2], ACT.Sigmoid)

            def decay(g, c):
                name = f"proj0_{c}"
                wait_filled(act, g, name)
                act.activation(gbank(name)[:, :], gbank(name)[:, :], ACT.Exp,
                               bias=v_("time_decay", c)).then_inc(doubled, 1)
                act.wait_ge(doubled, at(g, CT, c + 1))
                act.activation(w_sh[:, c, :, 1:P], b3(gbank(name)[:, :])[:, :, 0:P - 1], ACT.Exp,
                               scale=-1.0).then_inc(drained["act"], 1)

            def ahead(g, before=None):
                def prev(work, n):
                    if before is not None:
                        work(before, n)
                move(g, "lora0", th0[:, :], ACT.Tanh)
                wait_drained(act, g, "lora0")
                act.activation(parts[:, 0, :], th0[:, :], ACT.Copy).then_inc(part_high, 1)
                move(g, "lora1", th1[0:DM, :], ACT.Tanh, DM)
                prev(key, 0)
                move(g, "route_t0", routed[:, 0, :])
                prev(key, 1)
                move(g, "route_t2", routed[:, 2, :])
                prev(key, 2)
                prev(key, 3)
                move(g, "route_t1", routed[:, 1, :])
                prev(recept, 0)
                move(g, "route_t3", routed[:, 3, :])
                wait_filled(act, g, "route_t3")
                act.activation(parts[0:DM, 0, :], th1[0:DM, :], ACT.Copy).then_inc(part_high, 1)
                act.wait_ge(part_low, at(g, 2 + CT, 2))
                move(g, "decay_in", dl[0:DD, :], ACT.Tanh, DD)
                prev(recept, 1)
                move(g, "route_t4", routed[:, 0, :])
                take_v(g, 0)
                prev(recept, 2)
                move(g, "route_v0_0", routed[:, 0, :])
                prev(recept, 3)
                move(g, "route_v0_1", routed[:, 1, :])
                decay(g, 0)
                decay(g, 1)
                decay(g, 2)
                if before is not None:
                    act.wait_ge(gated, at(before, GB, GB - 1))
                move(g, "proj1_0", k_pad[:, 0, :, 1:P + 1])
                decay(g, 3)
                move(g, "proj3_0", r_sb[:, 0, :, :])

            def group(g):
                act.wait_ge(s0_landed, at(g, 16 * GB, 16 * GB))
                for m in range(STEPS):
                    c, j = m // S, m % S
                    act.wait_ge(bcast, at(g, STEPS, m + 1))
                    act.activation(vb[m % RING][:, :, 0], s0[:, :, c, 4 * (j % 4) + j // 4],
                                   ACT.Copy).then_inc(s0_put, 1)
                    last = c == CT - 1
                    if j == 3:
                        silu(g, 0) if last else take_v(g, c + 1)
                    if j == 5 and c:
                        center_square(g, c - 1)
                    if j == 9 and last:
                        silu(g, 1)
                    if j == 9 and not last:
                        if c + 1 >= 2:
                            act.wait_ge(kv, at(g, STEPS, c * S))
                        move(g, f"proj1_{c + 1}", k_pad[:, (c + 1) % 2, :, 1:P + 1])
                    if j == 9 and c:
                        load_table(ACT.Ln)
                    if j == 10 and c:
                        take_ln_var(g, c - 1)
                    if j == 11 and c:
                        load_table(ACT.Exp)
                    if j == 10 and not last:
                        move(g, f"route_v{c + 1}_0", routed[:, 2 * ((c + 1) % 2), :])
                    if j == 15 and not last:
                        move(g, f"route_v{c + 1}_1", routed[:, 2 * ((c + 1) % 2) + 1, :])
                    if j == 12 and c:
                        inverse_root(g, c - 1)
                    if j == 14:
                        silu(g, 2) if last else move(g, f"proj3_{c + 1}", r_sb[:, c + 1, :, :])
                silu(g, 3)
                center_square(g, CT - 1)
                load_table(ACT.Ln)
                take_ln_var(g, CT - 1)
                take_ln(g + 1, 0)
                inverse_root(g, CT - 1)
                take_rstd(g + 1, 0)
                load_table(ACT.Ln)
                act.activation(yg[:, :, :, 0], st_cols[:, :, 0, :], ACT.Copy).then_inc(edge[1], 1)
                act.wait_ge(edge[1], at(g, 1, 1))
                take_state(g + 1)
                first_norm(g + 1)
                take_ln(g, 1)
                take_rstd(g, 1)
                second_norm(g)
                ahead(g + 1, g)

            take_ln(0, 0)
            take_rstd(0, 0)
            take_state(0)
            first_norm(0)
            ahead(0)
            group(0)
            with act.Fori(1, NG) as g:
                group(g)

        @block.vector
        def _(dve):
            dve.memset(v_pad[:, :, :, :], 0.0).then_inc(preset, 1)
            dve.memset(eps[:, :], EPS).then_inc(preset, 1)
            dve.memset(k_pad[:, :, :, 0], 1.0).then_inc(preset, 1)
            dve.memset(rs[:, :], 0.0).then_inc(preset, 1)
            dve.memset(spare[:, :], 0.0).then_inc(preset, 1)
            dve.wait_ge(preset, 5)
            dve.wait_ge(vec_in, 16)

            def convert():
                dve.wait_ge(stage_in, 16 * 3)
                rt, rv, pick = (stage[1][:, a:b] for a, b in (
                    (C, C + ROUTE_T), (C + ROUTE_T, C + ROUTE_T + ROUTE_V),
                    (C + ROUTE_T + ROUTE_V, C + ROUTE_T + ROUTE_V + PICK)))
                dve.tensor_copy(spread[:, :, :], pick[:, :, None].broadcast_to((P, 64, S))).then_inc(converted, 1)
                dve.tensor_copy(route_t[:, :, :].rearrange("p f n -> p (f n)"), rt).then_inc(converted, 1)
                dve.tensor_copy(route_v[:, :, :].rearrange("p h n -> p (h n)"), rv).then_inc(converted, 1)
                w2_pieces = [(w2[:, 0:4, :].rearrange("p f n -> p (f n)"), stage[0]), (w2[:, 4, :], stage[1][:, 0:C])]
                for dst, src in w2_pieces:
                    dve.tensor_copy(dst, src).then_inc(converted, 1)
                dve.wait_ge(converted, 5)
                for dst, src in w2_pieces:
                    dve.tensor_tensor(dst[64:P], src[64:P], dst[64:P].bitcast(F32), ALU.subtract).then_inc(converted, 1)

            def statistics(n, rows, b):
                dve.bn_stats(stats[:, n, b, :], rows[:, b, :]).then_inc(stat[n], 1)

            def aggregate(g, n):
                dve.wait_ge(stat[n], at(g, 2 * GB, GB))
                dve.memset(spare[:, :], 0.0)
                for b in range(GB):
                    dve.bn_aggr(mv[:, n, b, :], stats[:, n, b, :]).then_inc(stat[n], 1)

            def normalise(g, n, rows):
                dve.wait_ge(rstd_done[n], at(g, 1, 1))
                for b in range(GB):
                    dve.tensor_scalar(xn[n][:, b, :], rows[:, b, :], mv[:, n, b, 0:1], rstd[:, n, b:b + 1],
                                      ALU.subtract, ALU.mult).then_inc(normed[n], 1)

            def first_statistics(g, b):
                dve.wait_ge(x_landed[b], at(g, 16, 16))
                statistics(0, x_in, b)

            def first_normalise(g):
                normalise(g, 0, x_in)
                dve.wait_ge(normed[0], at(g, GB, GB))
                dve.memset(w_sh[:, :, :, 0], 0.0).then_inc(zeroed, 1)

            def mix_x(g, c):
                if c == 0:
                    wait_filled(dve, g, f"tr1_{CT - 1}")
                dve.wait_ge(shifted, at(g, CT, c + 1))
                dve.scalar_tensor_tensor(out=b3(xxx[:, c, :]), in0=b3(sx[:, c, :]), scalar=v_("maa_x", c),
                                         in1=token_view[c], op0=ALU.mult, op1=ALU.add).then_inc(mixed_x, 1)

            def mix(g, f, half):
                name = ("maa_w", "maa_k", "maa_v", "maa_r", "maa_g")[f]
                for c in (2 * half, 2 * half + 1):
                    dve.wait_ge(mix_filled, mix_count(g, f, c))
                    if f == ORDER[0] and c == 0:
                        wait_if(dve, xr2_ready, at(g, CT, 0))
                    wait_if(dve, mixed[c % 2], reuse(g, NF * 2, ORDER.index(f) * 2 + c // 2, 2))
                    dve.scalar_tensor_tensor(out=mixt[:, c, :], in0=vb[c][:, :, :].rearrange("p b l -> p (b l)"),
                                             scalar=v_(name, c), in1=sx[:, c, :], op0=ALU.add,
                                             op1=ALU.mult).then_inc(mix_drained, 1)
                c = 2 * half + 1
                dve.wait_ge(mix_drained, mix_count(g, f, c))
                dve.tensor_tensor(b3(mixed_in[f][:, c, :]), b3(mixt[:, c, :]), token_view[c],
                                  ALU.add).then_inc(mixed[1], 1)

            def rest(g, n, rows, whole):
                dve.wait_ge(part_high, at(g, 2 + CT, n + 1))
                dst, high = parts[0:rows, 1, :], parts[0:rows, 0, :].bitcast(F32)
                if len(whole.shape) == 3:
                    dst, high = b3(dst), b3(high)
                dve.tensor_tensor(dst, whole, high, ALU.subtract).then_inc(part_low, 1)

            def take_y(g, c):
                dve.wait_ge(summed, at(g, STEPS, (c + 1) * S))
                dve.tensor_tensor(b3(y_sb[:, :]), b3(y_ps[:, :]), bon[c % 2], ALU.add).then_inc(y_done, 1)

            def scale_y(g, c):
                dve.wait_ge(rs_done, at(g, CT, c + 1))
                wait_drained(dve, g, f"center_{c}")
                dve.scalar_tensor_tensor(out=token_view2[c], in0=b3(y_sb[:, :]), scalar=v_("gn_w", c),
                                         in1=b3(rs[:, :]), op0=ALU.mult, op1=ALU.mult).then_inc(z_done, 1)

            def gate_y(g, c):
                dve.wait_ge(z_done, at(g, CT, c + 1))
                dve.wait_ge(gate_done, at(g, CT, c + 1))
                dve.scalar_tensor_tensor(out=token_view2[c], in0=token_view2[c], scalar=v_("gn_b", c),
                                         in1=b3(gbank(f"proj4_{c}")[:, :]), op0=ALU.add,
                                         op1=ALU.mult).then_inc(drained["dve"], 1)

            def residual(g, b):
                dve.wait_ge(wo_filled, at(g, GB, b + 1))
                dve.tensor_tensor(x1[:, b, :], vb[b][:, :, :].rearrange("p b l -> p (b l)"), x1[:, b, :],
                                  ALU.add).then_inc(residual_done, 1)
                dve.wait_ge(residual_done, at(g, GB, b + 1))

            def mix_key(g, c):
                dve.wait_ge(xc_done, at(g, CT, c + 1))
                dve.tensor_tensor(b3(sx2[:, c, :]), shifted_view2[c], token_view2[c],
                                  ALU.subtract).then_inc(shifted2, 1)
                dve.wait_ge(shifted2, at(g, CT, c + 1))
                dve.scalar_tensor_tensor(out=b3(xk2[:, c, :]), in0=b3(sx2[:, c, :]), scalar=v_("fmaa_k", c),
                                         in1=token_view2[c], op0=ALU.mult, op1=ALU.add).then_inc(xk2_ready, 1)

            def mix_recept(c):
                dve.scalar_tensor_tensor(out=b3(xr2[:, c, :]), in0=b3(sx2[:, c, :]), scalar=v_("fmaa_r", c),
                                         in1=token_view2[c], op0=ALU.mult, op1=ALU.add).then_inc(xr2_ready, 1)

            def finish(g, b):
                wait_filled(dve, g, f"value_{b}")
                wait_drained(dve, g, f"recept_{b}")
                dve.tensor_tensor(rr[:, b % 2], b3(gbank(f"value_{b}")[:, :]), rr[:, b % 2],
                                  ALU.mult).then_inc(drained["dve"], 1)
                wait_drained(dve, g, f"value_{b}")
                dve.tensor_tensor(b3(x1[:, b, :]), rr[:, b % 2], b3(x1[:, b, :]), ALU.add).then_inc(gated, 1)

            def ahead(g, before=None):
                def prev(b):
                    if before is not None:
                        finish(before, b)
                rest(g, 0, P, th0[:, :])
                if before is not None:
                    for c in range(CT):
                        mix_recept(c)
                mix(g, 0, 0)
                mix(g, 0, 1)
                rest(g, 1, DM, th1[0:DM, :])
                mix(g, 2, 0)
                prev(0)
                mix(g, 2, 1)
                mix(g, 1, 0)
                prev(1)
                mix(g, 1, 1)
                mix(g, 4, 0)
                rest(g, 2, P, v_pad[:, 0, :, 0:P])
                prev(2)
                mix(g, 4, 1)
                mix(g, 3, 0)
                prev(3)
                mix(g, 3, 1)

            def group(g):
                for m in range(STEPS + 1):
                    c, j = m // S, m % S
                    if m < STEPS:
                        if j == 0:
                            wait_drained(dve, g, f"proj1_{c}")
                        dve.wait_ge(s0_put, at(g, STEPS, m + 1))
                        dve.tensor_tensor(vb[m % RING][:, :, :], vb[m % RING][:, :, :], k_pad[:, c % 2, :, 0:P],
                                          ALU.mult).then_inc(kv, 1)
                    if m >= 1:
                        n = m - 1
                        if n == 0:
                            dve.wait_ge(zeroed, at(g, 1, 1))
                            for done in mixed:
                                dve.wait_ge(done, at(g, NF * 2, NF * 2))
                        if n % S == 0:
                            wait_drained(dve, g, f"proj0_{n // S}")
                        dve.wait_ge(kv, at(g, STEPS, n + 1))
                        wait_if(dve, prodded, reuse(g, STEPS, n, RING))
                        dve.tensor_tensor_scan(states[:, n % RING, :, :].rearrange("p b l -> p (b l)"),
                                               w_sh[:, n // S, :, :].rearrange("p b l -> p (b l)"),
                                               vb[n % RING][:, :, :].rearrange("p b l -> p (b l)"),
                                               0.0, ALU.mult, ALU.add).then_inc(scanned, 1)
                    if m == STEPS:
                        continue
                    if j == 0:
                        wait_drained(dve, g, f"proj3_{c}")
                        dve.scalar_tensor_tensor(out=rkf, in0=r_sb[:, c, :, :], scalar=v_("faaaa", c),
                                                 in1=k_pad[:, c % 2, :, 1:P + 1], op0=ALU.mult,
                                                 op1=ALU.mult).then_inc(bonus_in, 1)
                    if j == 3 and c >= 1:
                        take_y(g, c - 1)
                    if j == 6:
                        wait_filled(dve, g, f"bonus_{c}")
                        dve.tensor_tensor(bon[c % 2], b3(gbank(f"bonus_{c}")[:, :]), v_pad[:, c % 2, :, 1:P + 1],
                                          ALU.mult).then_inc(drained["dve"], 1)
                    if j == 14 and c >= 1:
                        scale_y(g, c - 1)
                    if j == 5 and c == CT - 1:
                        gate_y(g, 0)
                    if j == 11 and c == CT - 1:
                        gate_y(g, 1)
                for b in range(GB - 1):
                    first_statistics(g + 1, b)
                take_y(g, CT - 1)
                gate_y(g, 2)
                first_statistics(g + 1, GB - 1)
                aggregate(g + 1, 0)
                scale_y(g, CT - 1)
                gate_y(g, CT - 1)
                first_normalise(g + 1)
                dve.wait_ge(res_landed, at(g, 16, 16))
                for b in range(GB):
                    residual(g, b)
                    statistics(1, x1, b)
                aggregate(g, 1)
                mix_x(g + 1, 0)
                normalise(g, 1, x1)
                for c in range(1, CT):
                    mix_x(g + 1, c)
                dve.wait_ge(edge[1], at(g, 1, 1))
                for c in range(CT):
                    mix_key(g, c)
                ahead(g + 1, g)

            for b in range(GB):
                first_statistics(0, b)
            aggregate(0, 0)
            first_normalise(0)
            convert()
            for c in range(CT):
                mix_x(0, c)
            ahead(0)
            group(0)
            with dve.Fori(1, NG) as g:
                group(g)

        @block.gpsimd
        def _(pool):
            def shift(g):
                pool.wait_ge(edge[0], at(g, 1, 1))
                for c in range(CT):
                    wait_drained(pool, g, f"tr1_{c}")
                    pool.tensor_tensor(b3(sx[:, c, :]), shifted_view[c], token_view[c],
                                       ALU.subtract).then_inc(shifted, 1)

            def mix(g, f):
                for c in (0, 2):
                    pool.wait_ge(mix_drained, mix_count(g, f, c))
                    if c == 0 and f == 1:
                        wait_drained(pool, g, "lora1")
                    if c == 0 and f == 4:
                        wait_filled(pool, g, "decay_in")
                    pool.tensor_tensor(b3(mixed_in[f][:, c, :]), b3(mixt[:, c, :]), token_view[c],
                                       ALU.add).then_inc(mixed[0], 1)

            def ahead(g):
                shift(g)
                for f in ORDER:
                    mix(g, f)

            def group(g):
                for m in range(STEPS):
                    if m % S == 0:
                        wait_drained(pool, g, f"proj3_{m // S}")
                    pool.wait_ge(scanned, at(g, STEPS, m + 1))
                    wait_if(pool, summed, reuse(g, STEPS, m, PRING))
                    if m % S == 6 and m // S + 1 < CT:
                        c = m // S + 1
                        pool.wait_ge(part_high, at(g, 2 + CT, c + 3))
                        pool.tensor_tensor(b3(parts[:, 1, :]), v_pad[:, c % 2, :, 0:P],
                                           b3(parts[:, 0, :].bitcast(F32)), ALU.subtract).then_inc(part_low, 1)
                    pool.tensor_tensor(b3(prods[:, m % PRING, :]), states[:, m % RING, :, :],
                                       r_sb[:, m // S, :, :], ALU.mult).then_inc(prodded, 1)
                ahead(g + 1)
            ahead(0)
            group(0)
            with pool.Fori(1, NG) as g:
                group(g)


def kernel(**inputs):
    import numpy as np
    import concourse.bacc as bacc
    from concourse.bass_utils import run_bass_kernel_spmd

    def arr(name):
        return np.asarray(inputs["L0_xattn_" + name])

    def perm(a, axis):
        a = np.moveaxis(a, axis, 0)
        a = a.reshape(CT, HT, S, *a.shape[1:]).swapaxes(1, 2).reshape(a.shape)
        return np.moveaxis(a, 0, axis)

    def tiles(a):
        return np.ascontiguousarray(a.reshape(CT, P, -1).transpose(1, 0, 2))

    arrays = {"x": np.ascontiguousarray(inputs["x"]), "ctx_in": np.ascontiguousarray(inputs["ctx_2048"])}
    cols = [perm(arr(n), 0) if n in ("gn_w", "gn_b") else arr(n).reshape(C) for n in VECS]
    arrays["vecs"] = np.ascontiguousarray(np.stack(cols).reshape(len(VECS), CT, P).transpose(2, 0, 1))
    for n in MATS:
        w = arr(n).T
        if n in ("Wv", "Wg"):
            w = perm(w, 1)
        if n == "Wo":
            w = perm(w, 0)
        arrays["m_" + n] = tiles(w)
    arrays["maa_w1"] = tiles(arr("maa_w1"))
    arrays["maa_w2"] = np.tile(arr("maa_w2").transpose(1, 0, 2).reshape(DM, NF * C), (4, 1))
    arrays["decay_w1"] = tiles(arr("decay_w1"))
    arrays["decay_w2"] = np.zeros((P, C), np.float32)
    arrays["decay_w2"][0:DD] = arr("decay_w2")

    head_n, s_n = np.arange(P) // S, np.arange(P) % S
    head_y = np.arange(P) % HT
    same_ny = (head_n[:, None] == head_y[None, :])
    same_yy = (head_y[:, None] == head_y[None, :])
    local = np.arange(32)
    gather = np.stack([(local // HT == i)[None, :] & (head_n[:, None] == (local % HT)[None, :]) for i in range(4)], 1)
    consts = {"ident": np.eye(P), "gather": gather.reshape(P, 128),
              "headsum": same_ny, "center": np.eye(P) - same_yy / S, "headmean": same_yy / S}
    p, n5, n3 = np.arange(P)[:, None, None], np.arange(5 * DM), np.arange(3 * 64)
    rt = (p == DM * np.arange(4)[:, None] + n5 % DM) & (n5 // DM % 2 == 0)
    rv = (p == 64 * np.arange(2)[:, None] + n3 - 64) & (n3 // 64 == 1)
    pick = p[:, 0] % 64 == np.arange(PICK)
    arrays["routes"] = np.concatenate([rt.reshape(P, -1), rv.reshape(P, -1), pick], 1).astype(np.float32)
    for n in SELS:
        arrays["s_" + n] = np.ascontiguousarray(consts[n].astype(np.float32))

    nc = bacc.Bacc("TRN2", target_bir_lowering=False, num_devices=1)
    ap = {n: nc.dram_tensor("in_" + n, a.shape, F32, kind="ExternalInput").ap() for n, a in arrays.items()}
    shape = inputs["x"].shape
    out = nc.dram_tensor("out_y", shape, F32, kind="ExternalOutput").ap()
    rwkv_kernel(nc, ap["x"], ap["ctx_in"], ap["vecs"], {n: ap["m_" + n] for n in MATS}, ap["maa_w1"], ap["maa_w2"],
                ap["decay_w1"], ap["decay_w2"], {n: ap["s_" + n] for n in SELS}, ap["routes"], out)
    r = run_bass_kernel_spmd(nc, [{"in_" + n: a for n, a in arrays.items()}], core_ids=[0])
    return r.results[0]["out_y"]
```
